# Optimizing a Trainium2 kernel written in Bass

```python
import numpy as np
import jax
import jax.numpy as jnp

def _softmax(x, axis=-1):
    return jax.nn.softmax(x, axis=axis)

def _gelu(x):
    return jax.nn.gelu(x, approximate=True)

def _silu(x):
    return jax.nn.silu(x)

def _sigmoid(x):
    return jax.nn.sigmoid(x)

def _layernorm(x, axis=-1, eps=1e-05):
    m = jnp.mean(x, axis=axis, keepdims=True)
    v = jnp.var(x, axis=axis, keepdims=True)
    return (x - m) / jnp.sqrt(v + eps)

def _scatter_add(tgt, idx, src, axis=0):
    return tgt.at[idx].add(src)

def _segment_sum(src, seg, n):
    return jax.ops.segment_sum(src, seg, n)
kernel_name = 'mk_adaln_ffn_d4_seqx_r8_d56062'

def setup_inputs(seed: int=0):
    np.random.seed(seed)
    _w = jnp.asarray

    def _rec_inputs():
        import jax
        import jax.numpy as jnp
        _rk = jax.random.key(seed)
        x = -0.000125 + 0.9999 * jax.random.normal(jax.random.fold_in(_rk, 1), (64, 32, 512), jnp.float32)
        _lenS = 32 - jax.random.randint(jax.random.fold_in(_rk, 7), (64,), 0, max(1, 32 // 4) + 1, jnp.int32)
        _lenS2 = 32 - jax.random.randint(jax.random.fold_in(_rk, 8), (64,), 0, max(1, 32 // 4) + 1, jnp.int32)
        cond_128 = 0.0061147 + 1.02565 * jax.random.normal(jax.random.fold_in(_rk, 11), (64, 128), jnp.float32)
        fside_S_0 = -0.022604 + 0.987366 * jax.random.normal(jax.random.fold_in(_rk, 12), (32,), jnp.float32)
        return (x, cond_128, fside_S_0)
    x, cond_128, fside_S_0 = _rec_inputs()

    def _L0_cond_setup():
        import jax, jax.numpy as jnp
        import numpy as np
        K = 8
        T = 1.0
        D_EMBD = 128
        IN_C = 32
        OUT_C = 32
        BS = 32
        H = 512
        HID = 128
        key = jax.random.key(seed)
        ks = jax.random.split(key, 10)
        s = lambda fan_in: 1.0 / np.sqrt(fan_in)
        return {'x': jax.random.normal(ks[0], (BS, IN_C, H), dtype=jnp.float32), 'embedding': jax.random.normal(ks[1], (BS, D_EMBD), dtype=jnp.float32), 'W0': jax.random.normal(ks[2], (D_EMBD, HID), dtype=jnp.float32) * s(D_EMBD), 'b0': jnp.zeros((HID,), dtype=jnp.float32), 'W1': jax.random.normal(ks[3], (HID, HID), dtype=jnp.float32) * s(HID), 'b1': jnp.zeros((HID,), dtype=jnp.float32), 'W2': jax.random.normal(ks[4], (HID, K), dtype=jnp.float32) * s(HID), 'b2': jnp.zeros((K,), dtype=jnp.float32), 'weight': jax.random.normal(ks[5], (K, OUT_C, IN_C, 1), dtype=jnp.float32) * s(IN_C), 'bias_k': jax.random.normal(ks[6], (K, OUT_C), dtype=jnp.float32) * 0.1}
    _L0_cond_all = _L0_cond_setup()
    _L0_cond_in = {k: v for k, v in _L0_cond_all.items() if k in ('W0', 'b0', 'W1', 'b1', 'W2', 'b2', 'weight', 'bias_k')}
    del _L0_cond_all

    def _L0_ffn_setup():
        import jax, jax.numpy as jnp
        import numpy as np
        HD, M = (512, 1792)
        key = jax.random.key(seed)
        k_x, k_g, k_u, k_d = jax.random.split(key, 4)
        scale = 1.0 / np.sqrt(HD)
        x = jax.random.normal(k_x, (4, 256, HD), dtype=jnp.float16)
        W_gate = jax.random.normal(k_g, (M, HD), dtype=jnp.float16) * jnp.float16(scale)
        W_up = jax.random.normal(k_u, (M, HD), dtype=jnp.float16) * jnp.float16(scale)
        W_down = jax.random.normal(k_d, (HD, M), dtype=jnp.float16) * jnp.float16(1.0 / np.sqrt(M))
        return {'x': x, 'W_gate': W_gate, 'W_up': W_up, 'W_down': W_down}
    _L0_ffn_all = _L0_ffn_setup()
    _L0_ffn_in = {k: v for k, v in _L0_ffn_all.items() if k in ('W_gate', 'W_up', 'W_down')}
    del _L0_ffn_all

    def _L1_cond_setup():
        import jax, jax.numpy as jnp
        import numpy as np
        from jax import lax
        N, C_IN, L = (32, 32, 512)
        C_OUT, K, GROUPS = (32, 9, 4)
        C_DIM, PAD, STRIDE = (128, 4, 1)
        key = jax.random.key(seed)
        k1, k2, k3, k4, k5 = jax.random.split(key, 5)
        x = jax.random.normal(k1, (N, C_IN, L), dtype=jnp.float32)
        c = jax.random.normal(k2, (N, C_DIM), dtype=jnp.float32)
        weight = jax.random.normal(k3, (C_OUT, C_IN // GROUPS, K), dtype=jnp.float32)
        c_weight = jax.random.normal(k4, (C_OUT, C_DIM), dtype=jnp.float32)
        bias = jax.random.normal(k5, (C_OUT,), dtype=jnp.float32)
        return {'x': x, 'c': c, 'weight': weight, 'c_weight': c_weight, 'bias': bias}
    _L1_cond_all = _L1_cond_setup()
    _L1_cond_in = {k: v for k, v in _L1_cond_all.items() if k in ('weight', 'c_weight')}
    del _L1_cond_all

    def _L1_ffn_setup():
        import jax, jax.numpy as jnp
        import numpy as np
        D_IN = 512
        D_OUT = 512
        RANK = 16
        NUM_EXPERTS = 8
        TOP_K = 2
        SCALING = 32.0 / RANK
        key = jax.random.key(seed)
        ks = jax.random.split(key, 6)
        x = jax.random.normal(ks[0], (4, 256, D_IN), dtype=jnp.float32)
        W_base = jax.random.normal(ks[1], (D_OUT, D_IN), dtype=jnp.float32) * (1.0 / np.sqrt(D_IN))
        b_base = jax.random.normal(ks[2], (D_OUT,), dtype=jnp.float32) * 0.01
        W_router = jax.random.normal(ks[3], (NUM_EXPERTS, D_IN), dtype=jnp.float32) * 0.01
        A_stack = jax.random.uniform(ks[4], (NUM_EXPERTS, RANK, D_IN), dtype=jnp.float32, minval=-1.0, maxval=1.0) * (1.0 / np.sqrt(D_IN))
        B_stack = jax.random.normal(ks[5], (NUM_EXPERTS, D_OUT, RANK), dtype=jnp.float32) * 0.02
        return {'x': x, 'W_base': W_base, 'b_base': b_base, 'W_router': W_router, 'A_stack': A_stack, 'B_stack': B_stack}
    _L1_ffn_all = _L1_ffn_setup()
    _L1_ffn_in = {k: v for k, v in _L1_ffn_all.items() if k in ('W_base', 'b_base', 'W_router', 'A_stack', 'B_stack')}
    del _L1_ffn_all

    def _L2_cond_setup():
        import jax, jax.numpy as jnp
        import numpy as np
        K = 8
        T = 1.0
        D_EMBD = 128
        IN_C = 32
        OUT_C = 32
        BS = 32
        H = 512
        HID = 128
        key = jax.random.key(seed)
        ks = jax.random.split(key, 10)
        s = lambda fan_in: 1.0 / np.sqrt(fan_in)
        return {'x': jax.random.normal(ks[0], (BS, IN_C, H), dtype=jnp.float32), 'embedding': jax.random.normal(ks[1], (BS, D_EMBD), dtype=jnp.float32), 'W0': jax.random.normal(ks[2], (D_EMBD, HID), dtype=jnp.float32) * s(D_EMBD), 'b0': jnp.zeros((HID,), dtype=jnp.float32), 'W1': jax.random.normal(ks[3], (HID, HID), dtype=jnp.float32) * s(HID), 'b1': jnp.zeros((HID,), dtype=jnp.float32), 'W2': jax.random.normal(ks[4], (HID, K), dtype=jnp.float32) * s(HID), 'b2': jnp.zeros((K,), dtype=jnp.float32), 'weight': jax.random.normal(ks[5], (K, OUT_C, IN_C, 1), dtype=jnp.float32) * s(IN_C), 'bias_k': jax.random.normal(ks[6], (K, OUT_C), dtype=jnp.float32) * 0.1}
    _L2_cond_all = _L2_cond_setup()
    _L2_cond_in = {k: v for k, v in _L2_cond_all.items() if k in ('W0', 'b0', 'W1', 'b1', 'W2', 'b2', 'weight', 'bias_k')}
    del _L2_cond_all

    def _L2_ffn_setup():
        import jax, jax.numpy as jnp
        import numpy as np
        K_TOP = 8
        key = jax.random.key(seed)
        k1, k2, k3 = jax.random.split(key, 3)
        B, S, H, E = (4, 512, 512, 64)
        hidden_states = jax.random.normal(k1, (B, S, H), dtype=jnp.float32)
        router_weight = jax.random.normal(k2, (E, H), dtype=jnp.float32)
        router_bias = jnp.zeros((E,), dtype=jnp.float32)
        expert_bias = jax.random.normal(k3, (E, H), dtype=jnp.float32) * 0.1
        return {'hidden_states': hidden_states, 'router_weight': router_weight, 'router_bias': router_bias, 'expert_bias': expert_bias}
    _L2_ffn_all = _L2_ffn_setup()
    _L2_ffn_in = {k: v for k, v in _L2_ffn_all.items() if k in ('router_weight', 'router_bias', 'expert_bias')}
    del _L2_ffn_all

    def _L3_cond_setup():
        import jax, jax.numpy as jnp
        import numpy as np
        K = 8
        T = 1.0
        D_EMBD = 128
        IN_C = 32
        OUT_C = 32
        BS = 32
        H = 512
        HID = 128
        key = jax.random.key(seed)
        ks = jax.random.split(key, 10)
        s = lambda fan_in: 1.0 / np.sqrt(fan_in)
        return {'x': jax.random.normal(ks[0], (BS, IN_C, H), dtype=jnp.float32), 'embedding': jax.random.normal(ks[1], (BS, D_EMBD), dtype=jnp.float32), 'W0': jax.random.normal(ks[2], (D_EMBD, HID), dtype=jnp.float32) * s(D_EMBD), 'b0': jnp.zeros((HID,), dtype=jnp.float32), 'W1': jax.random.normal(ks[3], (HID, HID), dtype=jnp.float32) * s(HID), 'b1': jnp.zeros((HID,), dtype=jnp.float32), 'W2': jax.random.normal(ks[4], (HID, K), dtype=jnp.float32) * s(HID), 'b2': jnp.zeros((K,), dtype=jnp.float32), 'weight': jax.random.normal(ks[5], (K, OUT_C, IN_C, 1), dtype=jnp.float32) * s(IN_C), 'bias_k': jax.random.normal(ks[6], (K, OUT_C), dtype=jnp.float32) * 0.1}
    _L3_cond_all = _L3_cond_setup()
    _L3_cond_in = {k: v for k, v in _L3_cond_all.items() if k in ('W0', 'b0', 'W1', 'b1', 'W2', 'b2', 'weight', 'bias_k')}
    del _L3_cond_all

    def _L3_ffn_setup():
        import jax, jax.numpy as jnp
        import numpy as np

        @jax.custom_vjp
        def ste_sign(w):
            return jnp.sign(w)

        def _ste_fwd(w):
            return (jnp.sign(w), w)

        def _ste_bwd(w, g):
            mask = ((w > -1) & (w < 1)).astype(g.dtype)
            return (g * mask,)
        ste_sign.defvjp(_ste_fwd, _ste_bwd)
        key = jax.random.key(seed)
        k = jax.random.split(key, 6)
        B, S, H, O, E = (4, 256, 512, 512, 8)
        return {'x': jax.random.normal(k[0], (B, S, H), dtype=jnp.float32), 'weight': jax.random.normal(k[1], (O, H), dtype=jnp.float32) * 0.02, 'bias': jax.random.normal(k[2], (O,), dtype=jnp.float32) * 0.02, 'gate_w': jax.random.normal(k[3], (E, H), dtype=jnp.float32) * 0.02, 'in_channel_scale': jax.random.normal(k[4], (E, H), dtype=jnp.float32), 'out_channel_scale': jax.random.normal(k[5], (E, O), dtype=jnp.float32)}
    _L3_ffn_all = _L3_ffn_setup()
    _L3_ffn_in = {k: v for k, v in _L3_ffn_all.items() if k in ('weight', 'bias', 'gate_w', 'in_channel_scale', 'out_channel_scale')}
    del _L3_ffn_all
    return {'x': x, 'cond_128': cond_128, 'fside_S_0': fside_S_0, 'L0_cond_W0': _L0_cond_in['W0'], 'L0_cond_b0': _L0_cond_in['b0'], 'L0_cond_W1': _L0_cond_in['W1'], 'L0_cond_b1': _L0_cond_in['b1'], 'L0_cond_W2': _L0_cond_in['W2'], 'L0_cond_b2': _L0_cond_in['b2'], 'L0_cond_weight': _L0_cond_in['weight'], 'L0_cond_bias_k': _L0_cond_in['bias_k'], 'L0_ffn_W_gate': _L0_ffn_in['W_gate'], 'L0_ffn_W_up': _L0_ffn_in['W_up'], 'L0_ffn_W_down': _L0_ffn_in['W_down'], 'L1_cond_weight': _L1_cond_in['weight'], 'L1_cond_c_weight': _L1_cond_in['c_weight'], 'L1_ffn_W_base': _L1_ffn_in['W_base'], 'L1_ffn_b_base': _L1_ffn_in['b_base'], 'L1_ffn_W_router': _L1_ffn_in['W_router'], 'L1_ffn_A_stack': _L1_ffn_in['A_stack'], 'L1_ffn_B_stack': _L1_ffn_in['B_stack'], 'L2_cond_W0': _L2_cond_in['W0'], 'L2_cond_b0': _L2_cond_in['b0'], 'L2_cond_W1': _L2_cond_in['W1'], 'L2_cond_b1': _L2_cond_in['b1'], 'L2_cond_W2': _L2_cond_in['W2'], 'L2_cond_b2': _L2_cond_in['b2'], 'L2_cond_weight': _L2_cond_in['weight'], 'L2_cond_bias_k': _L2_cond_in['bias_k'], 'L2_ffn_router_weight': _L2_ffn_in['router_weight'], 'L2_ffn_router_bias': _L2_ffn_in['router_bias'], 'L2_ffn_expert_bias': _L2_ffn_in['expert_bias'], 'L3_cond_W0': _L3_cond_in['W0'], 'L3_cond_b0': _L3_cond_in['b0'], 'L3_cond_W1': _L3_cond_in['W1'], 'L3_cond_b1': _L3_cond_in['b1'], 'L3_cond_W2': _L3_cond_in['W2'], 'L3_cond_b2': _L3_cond_in['b2'], 'L3_cond_weight': _L3_cond_in['weight'], 'L3_cond_bias_k': _L3_cond_in['bias_k'], 'L3_ffn_weight': _L3_ffn_in['weight'], 'L3_ffn_bias': _L3_ffn_in['bias'], 'L3_ffn_gate_w': _L3_ffn_in['gate_w'], 'L3_ffn_in_channel_scale': _L3_ffn_in['in_channel_scale'], 'L3_ffn_out_channel_scale': _L3_ffn_in['out_channel_scale']}

def reference(x, cond_128, fside_S_0, L0_cond_W0, L0_cond_b0, L0_cond_W1, L0_cond_b1, L0_cond_W2, L0_cond_b2, L0_cond_weight, L0_cond_bias_k, L0_ffn_W_gate, L0_ffn_W_up, L0_ffn_W_down, L1_cond_weight, L1_cond_c_weight, L1_ffn_W_base, L1_ffn_b_base, L1_ffn_W_router, L1_ffn_A_stack, L1_ffn_B_stack, L2_cond_W0, L2_cond_b0, L2_cond_W1, L2_cond_b1, L2_cond_W2, L2_cond_b2, L2_cond_weight, L2_cond_bias_k, L2_ffn_router_weight, L2_ffn_router_bias, L2_ffn_expert_bias, L3_cond_W0, L3_cond_b0, L3_cond_W1, L3_cond_b1, L3_cond_W2, L3_cond_b2, L3_cond_weight, L3_cond_bias_k, L3_ffn_weight, L3_ffn_bias, L3_ffn_gate_w, L3_ffn_in_channel_scale, L3_ffn_out_channel_scale):
    import jax
    import jax.numpy as jnp

    def _L0_cond_ref(x, embedding, W0, b0, W1, b1, W2, b2, weight, bias_k):
        import jax, jax.numpy as jnp
        import numpy as np
        K = 8
        T = 1.0
        D_EMBD = 128
        IN_C = 32
        OUT_C = 32
        BS = 32
        H = 512
        HID = 128
        h = jax.nn.gelu(embedding @ W0 + b0, approximate=False)
        h = jax.nn.gelu(h @ W1 + b1, approximate=False)
        att = jax.nn.softmax((h @ W2 + b2) / T, axis=-1)
        agg_w = jnp.einsum('bk,koi->boi', att, weight[..., 0])
        agg_b = att @ bias_k
        out = jnp.einsum('boi,bih->boh', agg_w, x) + agg_b[:, :, None]
        return out

    def _L0_ffn_ref(x, W_gate, W_up, W_down):
        import jax, jax.numpy as jnp
        import numpy as np
        HD, M = (512, 1792)
        gate = jnp.einsum('bsh,mh->bsm', x, W_gate)
        up = jnp.einsum('bsh,mh->bsm', x, W_up)
        h = jax.nn.silu(gate) * up
        out = jnp.einsum('bsm,hm->bsh', h, W_down)
        return out

    def _L1_cond_ref(x, c, weight, c_weight, bias):
        import jax, jax.numpy as jnp
        import numpy as np
        from jax import lax
        N, C_IN, L = (32, 32, 512)
        C_OUT, K, GROUPS = (32, 9, 4)
        C_DIM, PAD, STRIDE = (128, 4, 1)
        out = lax.conv_general_dilated(x, weight, window_strides=(STRIDE,), padding=[(PAD, PAD)], dimension_numbers=('NCH', 'OIH', 'NCH'), feature_group_count=GROUPS)
        ctx = jnp.einsum('nd,od->no', c, c_weight)
        out = out + ctx[:, :, None] + bias[None, :, None]
        return out

    def _L1_ffn_ref(x, W_base, b_base, W_router, A_stack, B_stack):
        import jax, jax.numpy as jnp
        import numpy as np
        D_IN = 512
        D_OUT = 512
        RANK = 16
        NUM_EXPERTS = 8
        TOP_K = 2
        SCALING = 32.0 / RANK
        orig_shape = x.shape
        xf = x.reshape(-1, D_IN)
        logits = xf @ W_router.T
        probs = jax.nn.softmax(logits, axis=-1)
        topk_p, topk_i = jax.lax.top_k(probs, TOP_K)
        topk_p = topk_p / jnp.sum(topk_p, axis=-1, keepdims=True)
        combine = jnp.sum(jax.nn.one_hot(topk_i, NUM_EXPERTS, dtype=xf.dtype) * topk_p[..., None], axis=1)
        h = jnp.einsum('nd,erd->ner', xf, A_stack)
        h = h * combine[..., None]
        lora_out = jnp.einsum('ner,eor->no', h, B_stack) * SCALING
        base_out = xf @ W_base.T + b_base
        out = base_out + lora_out
        return out.reshape(orig_shape[:-1] + (D_OUT,))

    def _L2_cond_ref(x, embedding, W0, b0, W1, b1, W2, b2, weight, bias_k):
        import jax, jax.numpy as jnp
        import numpy as np
        K = 8
        T = 1.0
        D_EMBD = 128
        IN_C = 32
        OUT_C = 32
        BS = 32
        H = 512
        HID = 128
        h = jax.nn.gelu(embedding @ W0 + b0, approximate=False)
        h = jax.nn.gelu(h @ W1 + b1, approximate=False)
        att = jax.nn.softmax((h @ W2 + b2) / T, axis=-1)
        agg_w = jnp.einsum('bk,koi->boi', att, weight[..., 0])
        agg_b = att @ bias_k
        out = jnp.einsum('boi,bih->boh', agg_w, x) + agg_b[:, :, None]
        return out

    def _L2_ffn_ref(hidden_states, router_weight, router_bias, expert_bias):
        import jax, jax.numpy as jnp
        import numpy as np
        K_TOP = 8
        B, S, H = hidden_states.shape
        E = router_weight.shape[0]
        T = B * S
        flat = hidden_states.reshape(T, H)
        logits = jnp.einsum('th,eh->te', flat, router_weight) + router_bias
        scores = jax.nn.softmax(logits, axis=-1)
        topk_w, topk_idx = jax.lax.top_k(scores, K_TOP)
        w_sum = topk_w.sum(axis=-1, keepdims=True)
        w_dense = jnp.zeros((T, E), dtype=scores.dtype).at[jnp.arange(T)[:, None], topk_idx].add(topk_w)
        bias_mix = jnp.einsum('te,eh->th', w_dense, expert_bias)
        out = flat * w_sum + bias_mix
        return out.reshape(B, S, H)

    def _L3_cond_ref(x, embedding, W0, b0, W1, b1, W2, b2, weight, bias_k):
        import jax, jax.numpy as jnp
        import numpy as np
        K = 8
        T = 1.0
        D_EMBD = 128
        IN_C = 32
        OUT_C = 32
        BS = 32
        H = 512
        HID = 128
        h = jax.nn.gelu(embedding @ W0 + b0, approximate=False)
        h = jax.nn.gelu(h @ W1 + b1, approximate=False)
        att = jax.nn.softmax((h @ W2 + b2) / T, axis=-1)
        agg_w = jnp.einsum('bk,koi->boi', att, weight[..., 0])
        agg_b = att @ bias_k
        out = jnp.einsum('boi,bih->boh', agg_w, x) + agg_b[:, :, None]
        return out

    def _L3_ffn_ref(x, weight, bias, gate_w, in_channel_scale, out_channel_scale):
        import jax, jax.numpy as jnp
        import numpy as np

        @jax.custom_vjp
        def ste_sign(w):
            return jnp.sign(w)

        def _ste_fwd(w):
            return (jnp.sign(w), w)

        def _ste_bwd(w, g):
            mask = ((w > -1) & (w < 1)).astype(g.dtype)
            return (g * mask,)
        ste_sign.defvjp(_ste_fwd, _ste_bwd)
        B, S, H = x.shape
        xf = x.reshape(-1, H)
        router_logits = xf @ gate_w.T
        routing = jax.nn.softmax(router_logits.astype(jnp.float32), axis=1).astype(x.dtype)
        in_scale = routing @ in_channel_scale
        out_scale = routing @ out_channel_scale
        wb = ste_sign(weight)
        out = xf * in_scale @ wb.T * out_scale + bias
        return out.reshape(B, S, -1)
    x = x + _L0_ffn_ref(_L0_cond_ref(x, cond_128, L0_cond_W0, L0_cond_b0, L0_cond_W1, L0_cond_b1, L0_cond_W2, L0_cond_b2, L0_cond_weight, L0_cond_bias_k), L0_ffn_W_gate, L0_ffn_W_up, L0_ffn_W_down)
    x = x + _L1_ffn_ref(_L1_cond_ref(x, cond_128, L1_cond_weight, L1_cond_c_weight, fside_S_0), L1_ffn_W_base, L1_ffn_b_base, L1_ffn_W_router, L1_ffn_A_stack, L1_ffn_B_stack)
    x = x + _L2_ffn_ref(_L2_cond_ref(x, cond_128, L2_cond_W0, L2_cond_b0, L2_cond_W1, L2_cond_b1, L2_cond_W2, L2_cond_b2, L2_cond_weight, L2_cond_bias_k), L2_ffn_router_weight, L2_ffn_router_bias, L2_ffn_expert_bias)
    x = x + _L3_ffn_ref(_L3_cond_ref(x, cond_128, L3_cond_W0, L3_cond_b0, L3_cond_W1, L3_cond_b1, L3_cond_W2, L3_cond_b2, L3_cond_weight, L3_cond_bias_k), L3_ffn_weight, L3_ffn_bias, L3_ffn_gate_w, L3_ffn_in_channel_scale, L3_ffn_out_channel_scale)
    return x

_drawn_inputs = setup_inputs


def setup_inputs(seed=0):
    import zlib

    import numpy as np

    out = dict(_drawn_inputs(seed))
    spreads = {'L0_cond_b0': (0.0, 0.8),
     'L0_cond_b1': (0.0, 0.8),
     'L0_cond_b2': (0.0, 0.8),
     'L2_cond_b0': (0.0, 0.395),
     'L2_cond_b1': (0.0, 0.1),
     'L2_cond_b2': (0.0, 0.1),
     'L2_ffn_router_bias': (0.0, 2.0),
     'L3_cond_b0': (0.0, 0.1),
     'L3_cond_b1': (0.0, 0.1),
     'L3_cond_b2': (0.0, 0.1)}
    factors = {'L0_cond_bias_k': 5.849,
     'L1_ffn_b_base': 64.0,
     'L2_cond_bias_k': 8.0,
     'L2_ffn_router_weight': 5.463,
     'L2_ffn_expert_bias': 5.721,
     'L3_cond_bias_k': 6.075,
     'L3_ffn_bias': 200.0}
    for name, (base, spread) in spreads.items():
        noise = np.random.default_rng([zlib.crc32(name.encode()), seed]).standard_normal(out[name].shape)
        drawn = base * np.exp(spread * noise) if base else spread * noise
        out[name] = jnp.asarray(drawn.astype(out[name].dtype))
    for name, factor in factors.items():
        out[name] = (out[name] * factor).astype(out[name].dtype)
    return out
```

```python
from contextlib import ExitStack

import concourse.bass as bass
from concourse import mybir

F32 = mybir.dt.float32
F32R = mybir.dt.float32r
ALU = mybir.AluOpType
ACT = mybir.ActivationFunctionType
AX = mybir.AxisListType.X

P = 128
D = 512
S = D // P
ROWS = 32
NB = 64
TB = P // ROWS
NT = NB // TB
GT = 4
G = NT // GT
GB = GT * TB
TOK = GT * P
K = 8
HID = 128
FF = 1792
M = FF // P
E1, RANK, TOP1 = 8, 16, 2
LORA_SCALE = 32.0 / RANK
AR = E1 * RANK + E1
E2, TOP2 = 64, 8
E3 = 8
NPAD = 96
TAPS, PAD = 9, 4
CB = 3
ds = bass.ds


def build(nc, A, out):
    ctx = ExitStack()
    with ctx:
        def sb(name, shape, dt=F32):
            return ctx.enter_context(nc.sbuf_tensor(name, shape, dt))

        def sem(name):
            return ctx.enter_context(nc.semaphore(name))

        x_all = sb("x_all", [P, NT, D])
        xs = sb("xs", [P, GT, D])
        cT = sb("cT", [P, S, TOK])
        c_hi = sb("c_hi", [P, S, TOK], F32R)
        c_lo = sb("c_lo", [P, S, TOK], F32R)
        silu = sb("silu", [P, 2, TOK])
        hff = sb("hff", [P, 2, TOK])
        h_hi = sb("h_hi", [P, 2, TOK], F32R)
        h_lo = sb("h_lo", [P, 2, TOK], F32R)
        agg = sb("agg", [P, 3, NT, ROWS])
        prod = sb("prod", [P, GT, K, ROWS])
        wk = sb("wk", [P, 3, K, ROWS])
        kbias = sb("kbias", [P, 3, ROWS])
        kb_att = sb("kb_att", [P, 3, TB, ROWS])
        bmask = sb("bmask", [P, TB])
        tmask = sb("tmask", [P, NT])
        blk = sb("blk", [P, GT, P])
        rbias = sb("rbias", [P, GB * ROWS])
        bias_bc = sb("bias_bc", [P, TOK])
        ones = sb("ones", [P, P])
        ident = sb("ident", [P, P])
        w0 = sb("w0", [P, 3, 2 * HID + K + 2])
        b2 = sb("b2", [NB, 3 * K])
        condT = sb("condT", [P, NB])
        cwT = sb("cwT", [P, ROWS])
        fside = sb("fside", [P, ROWS])
        selrep = sb("selrep", [NB, P])
        jmask = sb("jmask", [NB, NT * K])
        h1 = sb("h1", [P, 3, NB])
        h2 = sb("h2", [P, 3, NB])
        att = sb("att", [NB, 3, K])
        att_m = sb("att_m", [NB, 3, NT * K])
        att_bc = sb("att_bc", [P, 3, NT * K])
        attT = sb("attT", [P, 3, TB])
        st0 = sb("st0", [NB, 2, 3])
        stg = sb("stg", [P, GB, P + 2])
        wconv = sb("wconv", [P, CB, P])

        scrap = sb("scrap", [P, 1])
        stat = sb("stat", [P, 4, GT])
        m8 = sb("m8", [P, GT, 8])
        t8 = sb("t8", [P, GT, 8])

        with ExitStack() as first:
            wgu = first.enter_context(nc.sbuf_tensor("wgu", [P, M, 2 * S * P], F32R))
            wdn = first.enter_context(nc.sbuf_tensor("wdn", [P, M, D], F32R))
        lg = sb("lg", [P, GT, E2])
        ex = sb("ex", [P, GT, E2])
        rest = sb("rest", [P, GT, E2])
        wbase = sb("wbase", [P, S, D])
        war = sb("war", [P, S, AR])
        wlb = sb("wlb", [P, D])
        bbase = sb("bbase", [P, D])
        hm = sb("hm", [P, GT, P])
        hmT = sb("hmT", [P, TOK])
        wr2 = sb("wr2", [P, S, NPAD])
        wr3 = sb("wr3", [P, S, NPAD])
        rb2 = sb("rb2", [P, E2])
        eb2 = sb("eb2", [P, D])
        wsg = sb("wsg", [P, S * D])
        bias3 = sb("bias3", [P, D])
        inc3 = sb("inc3", [P, D])
        outc3 = sb("outc3", [P, D])
        t1 = sb("t1", [P, GT, D])
        osc = sb("osc", [P, GT, D])
        neg = osc[:].rearrange("p j n -> p (j n)")
        wcat = sb("wcat", [P, GT, P])
        rcat = sb("rcat", [P, GT, P])
        eb_hi = sb("eb_hi", [P, D], F32R)
        eb_lo = sb("eb_lo", [P, D], F32R)
        sgn = sb("sgn", [P, S, D], F32R)
        in_hi = sb("in_hi", [P, D], F32R)
        in_lo = sb("in_lo", [P, D], F32R)
        out_hi = sb("out_hi", [P, D], F32R)
        out_lo = sb("out_lo", [P, D], F32R)
        wT = sb("wT", [P, TOK], F32R)

        ps = ctx.enter_context(nc.psum_tensor("ps", [P, 8, 512], F32))

        def bank(i):
            return ps[:, i, :]

        def acc(j):
            return bank(j)

        s_small = sem("s_small")
        s_x = sem("s_x")
        s_w0 = [sem(f"s_w0_{m}") for m in range(M)]
        s_conv = sem("s_conv")
        s_l1w = sem("s_l1w")
        s_l23w = sem("s_l23w")
        s_ones = sem("s_ones")
        s_pad = sem("s_pad")
        s_mlp = sem("s_mlp")
        s_gelu = sem("s_gelu")
        s_att = sem("s_att")
        s_aexp = sem("s_aexp")
        s_abc = sem("s_abc")
        s_abcv = sem("s_abcv")
        s_agg = [sem(f"s_agg{i}") for i in range(3)]
        s_dv = sem("s_dv")
        s_pl = sem("s_pl")
        s_xs = [sem(f"s_xs{i}") for i in range(4)]
        s_prep = [sem(f"s_prep{i}") for i in range(4)]
        s_bmm = [sem(f"s_bmm{i}") for i in range(4)]
        s_bbc = [sem(f"s_bbc{i}") for i in range(4)]
        s_cmm = [sem(f"s_cmm{i}") for i in range(4)]
        s_c = [sem(f"s_c{i}") for i in range(4)]
        s_y = [sem(f"s_y{i}") for i in range(4)]
        s_acc = [sem(f"s_acc{i}") for i in range(4)]
        s_chi, s_clo = sem("s_chi"), sem("s_clo")
        s_gate, s_up = sem("s_gate"), sem("s_up")
        s_silu, s_h, s_hhi, s_hlo = sem("s_silu"), sem("s_h"), sem("s_hhi"), sem("s_hlo")
        s_ar, s_lg1, s_ex1, s_hm = sem("s_ar"), sem("s_lg1"), sem("s_ex1"), sem("s_hm")
        s_tr1, s_hmT, s_xb1 = sem("s_tr1"), sem("s_hmT"), sem("s_xb1")
        s_r2, s_lg2, s_ex2, s_wc = sem("s_r2"), sem("s_lg2"), sem("s_ex2"), sem("s_wc")
        s_ct, s_t1, s_px = sem("s_ct"), sem("s_t1"), sem("s_px")
        s_tr2, s_wT = sem("s_tr2"), sem("s_wT")
        s_split = sem("s_split")
        s_r3, s_lg3, s_ex3, s_rc = sem("s_r3"), sem("s_lg3"), sem("s_ex3"), sem("s_rc")
        s_tr3, s_rT, s_in, s_os, s_osc = sem("s_tr3"), sem("s_rT"), sem("s_in"), sem("s_os"), sem("s_osc")
        s_xm, s_xhi, s_xlo = sem("s_xm"), sem("s_xhi"), sem("s_xlo")
        s_xb3, s_f3 = sem("s_xb3"), sem("s_f3")
        s_out = sem("s_out")
        NSMALL = 12

        block = ctx.enter_context(nc.Block())

        COND = {0: 0, 2: 1, 3: 2}

        @block.sync
        def _(sp):
            small = [(w0[:], A["mlp"]), (condT[:], A["condT"]), (b2[:], A["b2"]), (selrep[:], A["selrep"]),
                     (jmask[:], A["jmask"]), (wk[:], A["wk"]), (kbias[:], A["kbias"]), (ident[:], A["ident"]),
                     (cwT[:], A["cwT"]), (fside[:], A["fside"]), (tmask[:], A["tmask"]), (bmask[:], A["bmask"])]
            for dst, src in small:
                sp.dma_start(dst, src).then_inc(s_small, 16)
            xd = A["x"].rearrange("(j p) n -> p j n", p=P)
            sp.dma_start(xs[:], xd[:, 0:GT, :]).then_inc(s_xs[0], 16)
            sp.dma_start(x_all[:], xd).then_inc(s_x, 16)
            sp.dma_start(wconv[:], A["wconv"]).then_inc(s_conv, 16)
            with sp.Fori(1, G) as g:
                sp.wait_ge(s_cmm[0], g * S)
                sp.dma_start(xs[:], xd[:, ds(g * GT, GT), :]).then_inc(s_xs[0], 16)

            sp.wait_ge(s_up, G * M)
            for dst, src in ((war, "war"), (wbase, "wbase"), (bbase, "bbase"), (wlb, "wlb")):
                sp.dma_start(dst[:], A[src]).then_inc(s_l1w, 16)

            sp.wait_ge(s_pad, 1)
            for g in range(G):
                sp.wait_ge(s_y[0], (g + 1) * GT)
                sp.wait_ge(s_cmm[1], g * GT)
                for s in range(S):
                    for b in range(TB):
                        src = x_all[b * ROWS:(b + 1) * ROWS, ds(g * GT, GT), s * P:(s + 1) * P]
                        dst = stg[s * ROWS:(s + 1) * ROWS, b:GB:TB, 1:P + 1]
                        sp.dma_start(dst, src).then_inc(s_xs[1], 16)

            for dst, src in ((wr2[:], "wr2"), (rb2[:], "rb2"), (eb2[:], "eb2"), (wr3[:], "wr3"), (wsg[:], "wsg"),
                             (bias3[:], "bias3"), (inc3[:], "inc3"), (outc3[:], "outc3")):
                sp.dma_start(dst, A[src]).then_inc(s_l23w, 16)
            for l, last in ((2, 0), (3, 2)):
                sp.wait_ge(s_cmm[last], G * S)
                for g in range(G):
                    sp.wait_ge(s_y[l - 1], (g + 1) * GT)
                    sp.wait_ge(s_cmm[l], g * S)
                    sp.dma_start(xs[:], x_all[:, ds(g * GT, GT), :]).then_inc(s_xs[l], 16)
            od = out.rearrange("(j p) n -> p j n", p=P)
            with sp.Fori(0, G) as g:
                sp.wait_ge(s_y[3], (g + 1) * GT)
                sp.dma_start(od[:, ds(g * GT, GT), :], x_all[:, ds(g * GT, GT), :]).then_inc(s_out, 16)
            sp.wait_ge(s_out, 16 * G)

        @block.gpsimd
        def _(pool):
            pool.memset(ones[:], 1.0).then_inc(s_ones, 1)
            pool.memset(stg[:, :, 0:P + 2:P + 1], 0.0).then_inc(s_pad, 1)
            for m in range(M):
                pool.dma_start(wgu[:, m, :], A["wgu"][m]).then_inc(s_w0[m], 16)
                pool.dma_start(wdn[:, m, :], A["wdn"][m]).then_inc(s_w0[m], 16)
            chain = [0]

            def step(ins):
                chain[0] += 1
                ins.then_inc(s_pl, 1)
                pool.wait_ge(s_pl, chain[0])

            def mix(i, q):
                a = att_bc[:, i, q * GT * K:(q + 1) * GT * K].rearrange("p (j k) -> p j k", k=K)
                step(pool.tensor_tensor(prod[:], a.unsqueeze(3).broadcast_to([P, GT, K, ROWS]),
                                        wk[:, i].unsqueeze(1).broadcast_to([P, GT, K, ROWS]), ALU.mult))
                for n in (4, 2):
                    step(pool.tensor_tensor(prod[:, :, 0:n], prod[:, :, 0:n], prod[:, :, n:2 * n], ALU.add))
                pool.tensor_tensor(agg[:, i, q * GT:(q + 1) * GT], prod[:, :, 0], prod[:, :, 1],
                                   ALU.add).then_inc(s_agg[i], 1)
                pool.wait_ge(s_agg[i], q + 1)

            def prepare(l, g):
                if l == 1:
                    pool.wait_ge(s_cmm[0], G * S)
                    pool.wait_ge(s_bmm[1], g)
                    pool.tensor_tensor(rbias[:].rearrange("p (b o) -> p b o", o=ROWS),
                                       condT[:, ds(g * GB, GB)].unsqueeze(2).broadcast_to([P, GB, ROWS]),
                                       cwT[:].unsqueeze(1).broadcast_to([P, GB, ROWS]),
                                       ALU.mult).then_inc(s_prep[1], 1)
                    return
                i = COND[l]
                pool.wait_ge(s_bmm[l], g)
                pool.tensor_tensor(rbias[:].rearrange("p (j n) -> p j n", j=GT),
                                   kb_att[:, i].rearrange("p b o -> p (b o)").unsqueeze(1).broadcast_to([P, GT, P]),
                                   tmask[:, ds(g * GT, GT)].unsqueeze(2).broadcast_to([P, GT, P]),
                                   ALU.mult).then_inc(s_prep[l], 1)
                pool.wait_ge(s_cmm[l], g * S)
                pool.tensor_tensor(blk[:].rearrange("p j (b o) -> p j b o", b=TB),
                                   agg[:, i, ds(g * GT, GT)].unsqueeze(2).broadcast_to([P, GT, TB, ROWS]),
                                   bmask[:].unsqueeze(1).unsqueeze(3).broadcast_to([P, GT, TB, ROWS]),
                                   ALU.mult).then_inc(s_prep[l], 1)

            pool.wait_ge(s_small, 16 * NSMALL)
            pool.wait_ge(s_ones, 1)
            pool.wait_ge(s_abcv, 6)
            for i in range(3):
                ins = pool.tensor_tensor(kb_att[:, i], kbias[:, i].unsqueeze(1).broadcast_to([P, TB, ROWS]),
                                         attT[:, i].unsqueeze(2).broadcast_to([P, TB, ROWS]), ALU.mult)
            step(ins)
            mix(0, 0)
            prepare(0, 0)
            for q in range(1, G):
                mix(0, q)
            with pool.Fori(1, G) as g:
                prepare(0, g)
            for i in (1, 2):
                for q in range(G):
                    mix(i, q)
            prepare(1, 0)

            def base_bias(g):
                pool.wait_ge(s_l1w, 64)
                pool.wait_ge(s_xs[1], 256 * (g + 1))
                xg = x_all[:, ds(g * GT, GT), :]
                pool.tensor_tensor(xg, xg, bbase[:].unsqueeze(1).broadcast_to([P, GT, D]),
                                   ALU.add).then_inc(s_xb1, 1)

            with pool.Fori(1, G) as g:
                base_bias(g - 1)
                prepare(1, g)
            base_bias(G - 1)

            pool.wait_ge(s_bmm[1], G)
            prepare(2, 0)

            def add_scaled(g):
                for j in range(GT):
                    pool.wait_ge(s_t1, g * GT + j + 1)
                    pool.wait_ge(s_xs[2], (g + 1) * 16)
                    xg = x_all[:, ds(g * GT + j, 1), :]
                    pool.tensor_tensor(xg, xg, t1[:, j:j + 1, :], ALU.add).then_inc(s_px, 1)

            with pool.Fori(1, G) as g:
                prepare(2, g)
                add_scaled(g - 1)
            add_scaled(G - 1)
            prepare(3, 0)

            def bias_3(g):
                pool.wait_ge(s_xs[3], 16 * (g + 1))
                xg = x_all[:, ds(g * GT, GT), :]
                pool.tensor_tensor(xg, xg, bias3[:].unsqueeze(1).broadcast_to([P, GT, D]), ALU.add).then_inc(s_xb3, 1)

            def finish_3(g):
                for j in range(GT):
                    pool.wait_ge(s_f3, g * GT + j + 1)
                    xg = x_all[:, ds(g * GT + j, 1), :]
                    pool.tensor_tensor(xg, xg, t1[:, j:j + 1, :], ALU.add).then_inc(s_y[3], 1)

            bias_3(0)
            prepare(3, 1)
            with pool.Fori(1, G - 1) as g:
                bias_3(g)
                pool.wait_ge(s_xb3, g)
                finish_3(g - 1)
                prepare(3, g + 1)
            bias_3(G - 1)
            pool.wait_ge(s_xb3, G - 1)
            finish_3(G - 2)
            pool.wait_ge(s_xb3, G)
            finish_3(G - 1)

        @block.tensor
        def _(pe):
            def mm(o, l, r, start=True, stop=True):
                return pe.matmul(o, l, r, start=start, stop=stop)

            pe.wait_ge(s_small, 16 * NSMALL)
            for i in range(3):
                mm(bank(0)[:, i * NB:(i + 1) * NB], w0[:, i, 0:HID], condT[:]).then_inc(s_mlp, 1)
            for i in range(3):
                pe.wait_ge(s_gelu, i + 1)
                mm(bank(1)[:, i * NB:(i + 1) * NB], w0[:, i, HID:2 * HID], h1[:, i]).then_inc(s_mlp, 1)
            for i in range(3):
                pe.wait_ge(s_gelu, 4 + i)
                mm(bank(2)[0:NB, i * K:(i + 1) * K], h2[:, i], w0[:, i, 2 * HID:2 * HID + K]).then_inc(s_mlp, 1)
            for i in range(3):
                pe.wait_ge(s_att, 7 + i)
                mm(bank(3)[:, i * NT * K:(i + 1) * NT * K], selrep[:], att_m[:, i]).then_inc(s_abc, 1)
                mm(bank(4)[:, i * TB:(i + 1) * TB], att_m[:, i], selrep[:, 0:P:ROWS]).then_inc(s_abc, 1)

            def cond(l, g, banks, before):
                pe.wait_ge(s_prep[l], 2 * g + 1)
                before[0]()
                mm(bank(banks[0]), ones[:], rbias[:]).then_inc(s_bmm[l], 1)
                pe.wait_ge(s_xs[l], 16 * (g + 1))
                pe.wait_ge(s_prep[l], 2 * g + 2)
                for s in range(S):
                    before[1 + s]()
                    for j in range(GT):
                        ins = mm(bank(banks[1 + s])[:, j * P:(j + 1) * P], xs[:, j, s * P:(s + 1) * P], blk[:, j])
                    ins.then_inc(s_cmm[l], 1)

            def nothing():
                pass

            def gate_up(g, m):
                n = g * M + m
                if m == 0:
                    pe.wait_ge(s_clo, S * (g + 1))
                else:
                    pe.wait_ge(s_w0[m], 32)
                if m >= 2:
                    pe.wait_ge(s_h, n - 1)
                b = 4 + 2 * (m % 2)
                for u, done in ((0, s_gate), (1, s_up)):
                    for s in range(S):
                        w = wgu[:, m, (u * S + s) * P:(u * S + s + 1) * P]
                        for c in (c_hi, c_lo):
                            ins = mm(bank(b + u), w, c[:, s], start=s == 0 and c is c_hi, stop=s == S - 1 and c is c_lo)
                    ins.then_inc(done, 1)

            def down(g, m):
                pe.wait_ge(s_hlo, g * M + m + 1)
                if m == 0:
                    pe.wait_ge(s_y[0], g * GT)
                for j in range(GT):
                    cols = slice(j * P, (j + 1) * P)
                    mm(acc(j), h_hi[:, m % 2, cols], wdn[:, m], start=m == 0, stop=False)
                    ins = mm(acc(j), h_lo[:, m % 2, cols], wdn[:, m], start=False, stop=m == M - 1)
                    if m == M - 1:
                        ins.then_inc(s_acc[0], 1)

            def layer0(g, more):
                for m in range(M):
                    gate_up(g, m)
                    if m >= 1:
                        down(g, m - 1)
                if more:
                    cond(0, g + 1, [5, 4, 5, 6, 7],
                         [lambda: pe.wait_ge(s_h, g * M + M - 1), nothing,
                          lambda: pe.wait_ge(s_bbc[0], g + 2),
                          lambda: pe.wait_ge(s_h, g * M + M), nothing])
                down(g, M - 1)

            pe.wait_ge(s_ones, 1)
            pe.wait_ge(s_abcv, 6)
            cond(0, 0, [5, 4, 5, 6, 7], [nothing, nothing, lambda: pe.wait_ge(s_bbc[0], 1), nothing, nothing])
            pe.wait_ge(s_w0[0], 32)
            with pe.Fori(0, G - 1) as g:
                layer0(g, True)
            layer0(G - 1, False)

            def conv_bias(g, first):
                pe.wait_ge(s_prep[1], g + 1)
                pe.wait_ge(s_hm, g)
                mm(bank(7), ones[:], rbias[:]).then_inc(s_bmm[1], 1)

            def conv(g, j):
                if j == 0:
                    pe.wait_ge(s_xs[1], 256 * (g + 1))
                if j == GT - 1:
                    pe.wait_ge(s_bbc[1], g + 1)
                for b in range(TB):
                    for c in range(CB):
                        ins = mm(bank(4 + j)[:, b * P:(b + 1) * P], stg[:, j * TB + b, c:c + P], wconv[:, c],
                                 start=c == 0, stop=c == CB - 1)
                ins.then_inc(s_cmm[1], 1)

            def lora_a_router(g):
                pe.wait_ge(s_l1w, 64)
                for j in range(GT):
                    pe.wait_ge(s_c[1], GT * g + GT)
                    for s in range(S):
                        ins = mm(bank(4 + j)[:, 0:AR], cT[:, s, j * P:(j + 1) * P], war[:, s], s == 0, s == S - 1)
                ins.then_inc(s_ar, 1)

            def base(g):
                pe.wait_ge(s_y[1], GT * g)
                for j in range(GT):
                    for s in range(S):
                        mm(acc(j), cT[:, s, j * P:(j + 1) * P], wbase[:, s], s == 0, False)

            def turn_hm(g):
                for j in range(GT):
                    ins = pe.transpose(bank(4)[:, j * P:(j + 1) * P], hm[:, j], ident[:])
                ins.then_inc(s_tr1, 1)

            def lora_b(g):
                pe.wait_ge(s_hmT, g + 1)
                for j in range(GT):
                    mm(acc(j), hmT[:, j * P:(j + 1) * P], wlb[:], False, True).then_inc(s_acc[1], 1)

            pe.wait_ge(s_conv, 16)
            pe.wait_ge(s_pad, 1)
            pe.wait_ge(s_h, G * M)
            pe.wait_ge(s_y[0], G * GT)
            conv_bias(0, True)
            for j in range(GT):
                conv(0, j)

            def layer1(g, more):
                lora_a_router(g)
                base(g)
                if more:
                    conv_bias(g + 1, False)
                    for j in range(GT - 1):
                        conv(g + 1, j)
                    pe.wait_ge(s_c[1], GT * (g + 1) + 1)
                else:
                    pe.wait_ge(s_hm, g + 1)
                turn_hm(g)
                if more:
                    conv(g + 1, GT - 1)
                lora_b(g)

            with pe.Fori(0, G - 1) as g:
                layer1(g, True)
            layer1(G - 1, False)

            def cond2(g):
                cond(2, g, [5, 6, 7, 5, 4],
                     [nothing, nothing, nothing, lambda: pe.wait_ge(s_bbc[2], g + 1), lambda: pe.wait_ge(s_lg2, g)])

            def router2(g):
                pe.wait_ge(s_c[2], S * (g + 1))
                pe.wait_ge(s_y[2], GT * g)
                for j in range(GT):
                    for s in range(S):
                        ins = mm(bank(4)[:, j * P:j * P + NPAD], cT[:, s, j * P:(j + 1) * P], wr2[:, s], s == 0, s == S - 1)
                ins.then_inc(s_r2, 1)

            def turn_c(g):
                pe.wait_ge(s_t1, GT * g)
                for j in range(GT):
                    for s in range(S):
                        ins = pe.transpose(acc(j)[:, s * P:(s + 1) * P], cT[:, s, j * P:(j + 1) * P], ident[:])
                    ins.then_inc(s_ct, 1)

            MIX = [5, 7, 4, 6]

            def layer2(g, more):
                router2(g)
                turn_c(g)
                if more:
                    cond2(g + 1)
                pe.wait_ge(s_wc, g + 1)
                if more:
                    pe.wait_ge(s_c[2], S * (g + 2))
                for j in range(GT):
                    ins = pe.transpose(bank(6)[:, j * P:(j + 1) * P], wcat[:, j], ident[:])
                ins.then_inc(s_tr2, 1)
                pe.wait_ge(s_wT, g + 1)
                for j in range(GT):
                    mm(bank(MIX[j]), wT[:, j * P:(j + 1) * P], eb_hi[:], True, False)
                    mm(bank(MIX[j]), wT[:, j * P:(j + 1) * P], eb_lo[:], False, True).then_inc(s_acc[2], 1)

            cond2(0)
            pe.wait_ge(s_l23w, 16 * 8)
            pe.wait_ge(s_y[1], G * GT)
            pe.wait_ge(s_split, 4)
            with pe.Fori(0, G - 1) as g:
                layer2(g, True)
            layer2(G - 1, False)

            def cond3(g):
                pe.wait_ge(s_xm, S * g)
                cond(3, g, [5, 4, 5, 6, 7], [nothing, nothing, lambda: pe.wait_ge(s_bbc[3], g + 1), nothing, nothing])

            def router3(g):
                pe.wait_ge(s_c[3], S * (g + 1))
                for j in range(GT):
                    for s in range(S):
                        ins = mm(bank(4)[:, j * P:j * P + NPAD], cT[:, s, j * P:(j + 1) * P], wr3[:, s], s == 0, s == S - 1)
                ins.then_inc(s_r3, 1)

            def sign_product(g):
                pe.wait_ge(s_xlo, S * (g + 1))
                for j in range(GT):
                    pe.wait_ge(s_osc, GT * g + j + 1)
                    for s in range(S):
                        cols = slice(j * P, (j + 1) * P)
                        mm(acc(j), c_hi[:, s, cols], sgn[:, s], s == 0, False)
                        ins = mm(acc(j), c_lo[:, s, cols], sgn[:, s], False, s == S - 1)
                    ins.then_inc(s_acc[3], 1)

            def scales(g):
                pe.wait_ge(s_rc, g + 1)
                for j in range(GT):
                    ins = pe.transpose(bank(5)[:, j * P:(j + 1) * P], rcat[:, j], ident[:])
                ins.then_inc(s_tr3, 1)
                pe.wait_ge(s_rT, g + 1)
                for s in range(S):
                    mm(bank(4 + s), in_hi[:, s * P:(s + 1) * P], wT[:]).then_inc(s_in, 1)
                for j in range(GT):
                    pe.wait_ge(s_f3, GT * (g - 1) + j + 1) if not (isinstance(g, int) and g == 0) else None
                    mm(acc(j), wT[:, j * P:(j + 1) * P], out_hi[:]).then_inc(s_os, 1)

            pe.wait_ge(s_y[2], G * GT)
            pe.wait_ge(s_split, 8)
            cond3(0)
            router3(0)
            scales(0)
            cond3(1)
            with pe.Fori(1, G - 1) as g:
                router3(g)
                sign_product(g - 1)
                scales(g)
                cond3(g + 1)
            router3(G - 1)
            sign_product(G - 2)
            scales(G - 1)
            sign_product(G - 1)

        @block.scalar
        def _(act):
            act.wait_ge(s_small, 16 * NSMALL)
            for n, (src, dst) in enumerate(((bank(0), h1), (bank(1), h2))):
                act.wait_ge(s_mlp, 3 * n + 3)
                for i in range(3):
                    b = w0[:, i, 2 * HID + K + n:2 * HID + K + n + 1]
                    act.activation(dst[:, i], src[:, i * NB:(i + 1) * NB], ACT.Gelu, bias=b).then_inc(s_gelu, 1)
            act.wait_ge(s_att, 3)
            act.activation(att[:], att[:], ACT.Exp).then_inc(s_aexp, 1)
            act.wait_ge(s_abc, 6)
            for i in range(3):
                act.activation(att_bc[:, i], bank(3)[:, i * NT * K:(i + 1) * NT * K], ACT.Copy).then_inc(s_abcv, 1)
                act.activation(attT[:, i], bank(4)[:, i * TB:(i + 1) * TB], ACT.Copy).then_inc(s_abcv, 1)

            def bias(l, g, b):
                act.wait_ge(s_bmm[l], g + 1)
                act.wait_ge(s_c[l], g * S)
                act.activation(bias_bc[:], bank(b), ACT.Copy).then_inc(s_bbc[l], 1)

            def split_c(g):
                for s in range(S):
                    act.wait_ge(s_c[0], S * g + s + 1)
                    act.activation(c_hi[:, s], cT[:, s], ACT.Copy).then_inc(s_chi, 1)

            def layer0(g, more):
                for m in range(M):
                    n = g * M + m
                    act.wait_ge(s_gate, n + 1)
                    act.activation(silu[:, m % 2], bank(4 + 2 * (m % 2)), ACT.Silu).then_inc(s_silu, 1)
                    act.wait_ge(s_h, n + 1)
                    act.activation(h_hi[:, m % 2], hff[:, m % 2], ACT.Copy).then_inc(s_hhi, 1)
                if more:
                    bias(0, g + 1, 5)
                    split_c(g + 1)

            bias(0, 0, 5)
            split_c(0)
            with act.Fori(0, G - 1) as g:
                layer0(g, True)
            layer0(G - 1, False)

            def exp(s_in, s_done, g, width):
                act.wait_ge(s_in, g + 1)
                act.activation(ex[:, :, 0:width], lg[:, :, 0:width], ACT.Exp).then_inc(s_done, 1)

            def layer1(g):
                exp(s_lg1, s_ex1, g, E1)
                act.wait_ge(s_tr1, g + 1)
                act.activation(hmT[:], bank(4), ACT.Copy).then_inc(s_hmT, 1)

            with act.Fori(0, G) as g:
                layer1(g)

            act.wait_ge(s_c[1], G * GT)
            bias(2, 0, 5)

            def layer2(g, more):
                exp(s_lg2, s_ex2, g, E2)
                if more:
                    bias(2, g + 1, 5)
                act.wait_ge(s_wc, g + 1)
                act.wait_ge(s_px, GT * g)
                for j in range(GT):
                    act.wait_ge(s_ct, GT * g + j + 1)
                    act.activation(t1[:, j], acc(j), ACT.Copy, scale=stat[:, 3, j:j + 1]).then_inc(s_t1, 1)
                act.wait_ge(s_tr2, g + 1)
                act.activation(wT[:], bank(6), ACT.Copy).then_inc(s_wT, 1)

            with act.Fori(0, G - 1) as g:
                layer2(g, True)
            layer2(G - 1, False)

            def scales(g):
                exp(s_lg3, s_ex3, g, E3)
                act.wait_ge(s_tr3, g + 1)
                act.activation(wT[:], bank(5), ACT.Copy).then_inc(s_rT, 1)
                for s in range(S):
                    act.wait_ge(s_xm, S * g + s + 1)
                    act.activation(c_hi[:, s], cT[:, s], ACT.Copy).then_inc(s_xhi, 1)
                for j in range(GT):
                    act.wait_ge(s_os, GT * g + j + 1)
                    act.activation(osc[:, j], acc(j), ACT.Copy).then_inc(s_osc, 1)

            act.wait_ge(s_acc[2], G * GT)
            bias(3, 0, 5)
            scales(0)
            bias(3, 1, 5)
            with act.Fori(1, G - 1) as g:
                scales(g)
                bias(3, g + 1, 5)
            scales(G - 1)

        @block.vector
        def _(dve):
            def tt(o, a, b, op):
                return dve.tensor_tensor(o, a, b, op)

            flat = att[:].rearrange("b i k -> b (i k)")
            dve.wait_ge(s_small, 16 * NSMALL)
            dve.wait_ge(s_mlp, 9)
            tt(flat, bank(2)[0:NB, 0:3 * K], b2[:], ALU.add).then_inc(s_att, 1)
            dve.wait_ge(s_att, 1)
            dve.tensor_reduce(st0[:, 0], att[:], AX, ALU.max).then_inc(s_att, 1)
            dve.wait_ge(s_att, 2)
            tt(att[:], att[:], st0[:, 0].unsqueeze(2).broadcast_to([NB, 3, K]), ALU.subtract).then_inc(s_att, 1)
            dve.wait_ge(s_aexp, 1)
            dve.tensor_reduce(st0[:, 0], att[:], AX, ALU.add).then_inc(s_att, 1)
            dve.wait_ge(s_att, 4)
            dve.reciprocal(st0[:, 1], st0[:, 0]).then_inc(s_att, 1)
            dve.wait_ge(s_att, 5)
            tt(att[:], att[:], st0[:, 1].unsqueeze(2).broadcast_to([NB, 3, K]), ALU.mult).then_inc(s_att, 1)
            dve.wait_ge(s_att, 6)
            for i in range(3):
                tt(att_m[:, i].rearrange("b (j k) -> b j k", k=K), jmask[:].rearrange("b (j k) -> b j k", k=K),
                   att[:, i].unsqueeze(1).broadcast_to([NB, NT, K]), ALU.mult).then_inc(s_att, 1)

            def cond(l, g, banks, split=None):
                dve.wait_ge(s_bbc[l], g + 1)
                for s in range(S + 1):
                    if s < S:
                        dve.wait_ge(s_cmm[l], S * g + s + 1)
                        tt(cT[:, s], bank(banks[s]), bias_bc[:], ALU.add).then_inc(s_c[l], 1)
                    if split and s >= 1:
                        split(g, s - 1)

            def split_c(g, s):
                dve.wait_ge(s_chi, S * g + s + 1)
                tt(c_lo[:, s], cT[:, s], c_hi[:, s].bitcast(F32), ALU.subtract).then_inc(s_clo, 1)

            def layer0(g, more):
                for m in range(M):
                    n = g * M + m
                    dve.wait_ge(s_silu, n + 1)
                    dve.wait_ge(s_up, n + 1)
                    tt(hff[:, m % 2], silu[:, m % 2], bank(5 + 2 * (m % 2)), ALU.mult).then_inc(s_h, 1)
                    dve.wait_ge(s_hhi, n + 1)
                    tt(h_lo[:, m % 2], hff[:, m % 2], h_hi[:, m % 2].bitcast(F32), ALU.subtract).then_inc(s_hlo, 1)
                if more:
                    cond(0, g + 1, [4, 5, 6, 7], split_c)
                for j in range(GT):
                    dve.wait_ge(s_acc[0], g * GT + j + 1)
                    xt = x_all[:, ds(g * GT + j, 1), :]
                    tt(xt, xt, acc(j).unsqueeze(1), ALU.add).then_inc(s_y[0], 1)

            cond(0, 0, [4, 5, 6, 7], split_c)
            dve.wait_ge(s_x, 16)
            with dve.Fori(0, G - 1) as g:
                layer0(g, True)
            layer0(G - 1, False)

            dn = [0]

            def cond1(g):
                dve.wait_ge(s_bmm[1], g + 1)
                v = bias_bc[:].rearrange("p (b o) -> p b o", o=ROWS)
                tt(v, bank(7).rearrange("p (b o) -> p b o", o=ROWS),
                   fside[:].unsqueeze(1).broadcast_to([P, GB, ROWS]), ALU.add).then_inc(s_bbc[1], 1)
                dve.wait_ge(s_bbc[1], g + 1)
                for j in range(GT):
                    dve.wait_ge(s_cmm[1], GT * g + j + 1)
                    o = cT[:, :, j * P:(j + 1) * P].rearrange("p s (b o) -> p b s o", o=ROWS)
                    tt(o, bank(4 + j).rearrange("p (b s o) -> p b s o", b=TB, s=S),
                       v[:, j * TB:(j + 1) * TB].unsqueeze(2).broadcast_to([P, TB, S, ROWS]), ALU.add).then_inc(s_c[1], 1)

            def bc(v, n):
                return v.unsqueeze(2).broadcast_to([P, GT, n])

            def alone():
                dve.memset(scrap[:], 0.0)

            def softmax_head(src, width, g, s_done, s_exp, first, link):
                link(dve.tensor_reduce(stat[:, 0], src, AX, ALU.max))
                tt(lg[:, :, 0:width], src, bc(stat[:, 0], width), ALU.subtract).then_inc(s_done, 1)
                dve.wait_ge(s_exp, g + 1)
                alone()

            def linker(s, base, per, g):
                n = [0]

                def link(ins, apart=False):
                    n[0] += 1
                    ins.then_inc(s, 1)
                    dve.wait_ge(s, base + per * g + n[0])
                    if apart:
                        alone()
                link.count = n
                return link

            PER1 = 9

            def route1(g):
                link = linker(s_dv, 0, PER1, g)
                dve.wait_ge(s_ar, g + 1)
                head = ps[:, 4:8, E1 * RANK:AR]
                softmax_head(head, E1, g, s_lg1, s_ex1, False, link)
                e = ex[:, :, 0:E1]
                for j in range(GT):
                    ins = dve.max(m8[:, j], ex[:, j, 0:E1])
                link(ins)
                link(dve.tensor_copy(t8[:, :, 0:TOP1], m8[:, :, 0:TOP1]), True)
                for j in range(GT):
                    ins = dve.match_replace(rest[:, j, 0:E1], t8[:, j], ex[:, j, 0:E1], 0.0)
                link(ins)
                link(tt(stat[:, 1], m8[:, :, 0], m8[:, :, 1], ALU.add))
                link(tt(lg[:, :, 0:E1], e, rest[:, :, 0:E1], ALU.subtract))
                link(dve.reciprocal(stat[:, 2], stat[:, 1]))
                link(dve.tensor_scalar(stat[:, 2], stat[:, 2], LORA_SCALE, None, ALU.mult))
                link(tt(lg[:, :, 0:E1], lg[:, :, 0:E1], bc(stat[:, 2], E1), ALU.mult))
                assert link.count[0] == PER1
                h = ps[:, 4:8, 0:E1 * RANK].rearrange("p j (e r) -> p j e r", r=RANK)
                tt(hm[:].rearrange("p j (e r) -> p j e r", r=RANK), h,
                   lg[:, :, 0:E1].unsqueeze(3).broadcast_to([P, GT, E1, RANK]), ALU.mult).then_inc(s_hm, 1)

            dve.memset(t8[:], -1.0).then_inc(s_pad, 1)
            dve.wait_ge(s_pad, 2)
            cond1(0)

            def residual(l, g, src):
                for j in range(GT):
                    dve.wait_ge(s_acc[l], GT * g + j + 1)
                    xt = x_all[:, ds(g * GT + j, 1), :]
                    tt(xt, xt, bank(src[j]).unsqueeze(1), ALU.add).then_inc(s_y[l], 1)

            with dve.Fori(0, G - 1) as g:
                route1(g)
                cond1(g + 1)
                dve.wait_ge(s_xb1, g + 1)
                residual(1, g, range(GT))
            route1(G - 1)
            dve.wait_ge(s_xb1, G)
            residual(1, G - 1, range(GT))

            dve.wait_ge(s_l23w, 16 * 8)
            dve.tensor_copy(eb_hi[:], eb2[:]).then_inc(s_split, 1)
            dve.tensor_copy(out_lo[:], outc3[:]).then_inc(s_split, 1)
            dve.tensor_copy(in_lo[:], inc3[:]).then_inc(s_split, 1)
            dve.wait_ge(s_split, 3)
            tt(eb_lo[:], eb2[:], eb_hi[:].bitcast(F32), ALU.subtract).then_inc(s_split, 1)

            cond(2, 0, [6, 7, 5, 4])

            PER2 = 9
            base2 = PER1 * G

            def route2(g):
                link = linker(s_dv, base2, PER2, g)
                dve.wait_ge(s_r2, g + 1)
                lt = bank(4).rearrange("p (j e) -> p j e", j=GT)[:, :, 0:E2]
                link(tt(lg[:], lt, rb2[:].unsqueeze(1).broadcast_to([P, GT, E2]), ALU.add))
                link(dve.tensor_reduce(stat[:, 0], lg[:], AX, ALU.max))
                tt(lg[:], lg[:], bc(stat[:, 0], E2), ALU.subtract).then_inc(s_lg2, 1)
                dve.wait_ge(s_ex2, g + 1)
                link(dve.tensor_reduce(stat[:, 1], ex[:], AX, ALU.add))
                link(dve.reciprocal(stat[:, 2], stat[:, 1]))
                link(tt(ex[:], ex[:], bc(stat[:, 2], E2), ALU.mult), True)
                for j in range(GT):
                    ins = dve.max(m8[:, j], ex[:, j])
                link(ins, True)
                for j in range(GT):
                    ins = dve.match_replace(rest[:, j], m8[:, j], ex[:, j], 0.0)
                link(ins)
                dve.wait_ge(s_t1, GT * g)
                dve.tensor_reduce(stat[:, 3], m8[:], AX, ALU.add)
                link(tt(lg[:], ex[:], rest[:], ALU.subtract))
                link(dve.tensor_copy(wcat[:, :, 0:E2].bitcast(F32R), lg[:]))
                tt(wcat[:, :, E2:2 * E2], lg[:], wcat[:, :, 0:E2], ALU.subtract).then_inc(s_wc, 1)
                assert link.count[0] == PER2

            MIX = [5, 7, 4, 6]

            def final2(g):
                for j in range(GT):
                    dve.wait_ge(s_acc[2], GT * g + j + 1)
                    dve.wait_ge(s_px, GT * g + j + 1)
                    xt = x_all[:, ds(g * GT + j, 1), :]
                    tt(xt, xt, bank(MIX[j]).unsqueeze(1), ALU.add).then_inc(s_y[2], 1)

            with dve.Fori(0, G - 1) as g:
                route2(g)
                cond(2, g + 1, [6, 7, 5, 4])
                final2(g)
            route2(G - 1)

            half = P // 2
            tt(in_hi[half:P], inc3[half:P], in_lo[half:P].bitcast(F32), ALU.subtract).then_inc(s_split, 1)
            tt(out_hi[half:P], outc3[half:P], out_lo[half:P].bitcast(F32), ALU.subtract).then_inc(s_split, 1)
            dve.tensor_copy(in_hi[0:half], inc3[0:half])
            dve.tensor_copy(out_hi[0:half], outc3[0:half]).then_inc(s_split, 1)
            link = linker(s_dv, base2 + PER2 * G, 1, 0)
            link(dve.tensor_scalar(neg, wsg[:], 0.0, None, ALU.is_lt))
            dve.scalar_tensor_tensor(sgn[:].rearrange("p s n -> p (s n)"), wsg[:], 0.0, neg, ALU.is_gt,
                                     ALU.subtract).then_inc(s_split, 1)
            final2(G - 1)

            dve.memset(rcat[:], 0.0)
            PER3 = 6
            base3 = base2 + PER2 * G + 1

            def route3(g):
                link = linker(s_dv, base3, PER3, g)
                dve.wait_ge(s_r3, g + 1)
                lt = bank(4).rearrange("p (j e) -> p j e", j=GT)[:, :, 0:E3]
                softmax_head(lt, E3, g, s_lg3, s_ex3, False, link)
                e = ex[:, :, 0:E3]
                link(dve.tensor_reduce(stat[:, 1], e, AX, ALU.add))
                link(dve.reciprocal(stat[:, 2], stat[:, 1]))
                link(tt(e, e, bc(stat[:, 2], E3), ALU.mult))
                r4 = rcat[:].rearrange("p j (q k) -> p j q k", q=4)
                for q in (0, 2):
                    ins = dve.tensor_copy(r4[:, :, q, 0:E3].bitcast(F32R), e)
                link(ins)
                link(tt(r4[:, :, 1, 0:E3], e, r4[:, :, 0, 0:E3], ALU.subtract))
                assert link.count[0] == PER3
                tt(r4[:, :, 3, 0:E3], e, r4[:, :, 0, 0:E3], ALU.subtract).then_inc(s_rc, 1)

            def scale_in(g):
                for s in range(S + 1):
                    if s < S:
                        dve.wait_ge(s_in, S * g + s + 1)
                        tt(cT[:, s], cT[:, s], bank(4 + s), ALU.mult).then_inc(s_xm, 1)
                    if s >= 1:
                        dve.wait_ge(s_xhi, S * g + s)
                        tt(c_lo[:, s - 1], cT[:, s - 1], c_hi[:, s - 1].bitcast(F32), ALU.subtract).then_inc(s_xlo, 1)

            def scale_out(g):
                dve.wait_ge(s_y[3], GT * g)
                for j in range(GT):
                    dve.wait_ge(s_acc[3], GT * g + j + 1)
                    tt(t1[:, j], osc[:, j], acc(j), ALU.mult).then_inc(s_f3, 1)

            cond(3, 0, [4, 5, 6, 7])
            route3(0)
            scale_in(0)
            dve.wait_ge(s_xlo, S)
            cond(3, 1, [4, 5, 6, 7])
            with dve.Fori(1, G - 1) as g:
                route3(g)
                scale_out(g - 1)
                scale_in(g)
                dve.wait_ge(s_xlo, S * (g + 1))
                cond(3, g + 1, [4, 5, 6, 7])
            route3(G - 1)
            scale_out(G - 2)
            scale_in(G - 1)
            scale_out(G - 1)


def kernel(**inputs):
    import numpy as np
    import concourse.bacc as bacc
    from concourse.bass_utils import run_bass_kernel_spmd as launch

    v = {n: np.asarray(a) for n, a in inputs.items()}

    def cols(a):
        return a.reshape(*a.shape[:-1], P, S).swapaxes(-1, -2).reshape(a.shape)

    def rows(a):
        return a.reshape(P, S, a.shape[-1])

    def everywhere(a):
        return np.broadcast_to(a, (P, *a.shape))

    conds = ("L0_cond_", "L2_cond_", "L3_cond_")

    def padded(a, n):
        o = np.zeros((*a.shape[:-1], n), a.dtype)
        o[..., :a.shape[-1]] = a
        return o

    mlp = np.stack([np.concatenate([v[c + "W0"], v[c + "W1"], v[c + "W2"], v[c + "b0"][:, None],
                                    v[c + "b1"][:, None]], 1) for c in conds], 1)
    b2 = np.broadcast_to(np.concatenate([v[c + "b2"] for c in conds]), (NB, 3 * K))
    wk = np.stack([np.tile(v[c + "weight"][..., 0].transpose(2, 0, 1), (TB, 1, 1)) for c in conds], 1)
    kbias = np.stack([np.tile(v[c + "bias_k"], (NT, 1)) for c in conds], 1)
    tmask = np.repeat(np.eye(NT, dtype=np.float32), K, 0)
    selrep = np.zeros((NB, TB, ROWS), np.float32)
    selrep[np.arange(NB), np.arange(NB) % TB] = 1
    jmask = np.zeros((NB, NT, K), np.float32)
    jmask[np.arange(NB), np.arange(NB) // TB] = 1
    cw = v["L1_cond_weight"]
    wconv = np.zeros((S, ROWS, CB, S, ROWS), np.float32)
    ig = cw.shape[1]
    for r in range(S):
        for tap in range(TAPS):
            at = r + tap - PAD + S
            for o in range(ROWS):
                i0 = o // ig * ig
                wconv[at % S, i0:i0 + ig, at // S, r, o] = cw[o, :, tap]

    def four(a):
        o = np.zeros((4, P // 4, a.shape[1]), a.dtype)
        o[:, :a.shape[0]] = a
        return o.reshape(P, -1)

    gu = np.stack([v["L0_ffn_W_gate"], v["L0_ffn_W_up"]])
    gu = gu.reshape(2, M, P, P, S).transpose(1, 3, 0, 4, 2).reshape(M, P, 2 * S * P)
    dn = cols(np.ascontiguousarray(v["L0_ffn_W_down"].T)).reshape(M, P, D)
    a_r = np.concatenate([v["L1_ffn_A_stack"].reshape(E1 * RANK, D), v["L1_ffn_W_router"]])
    host = {
        "x": cols(v["x"].reshape(NB * ROWS, D)),
        "mlp": mlp, "condT": v["cond_128"].T, "b2": b2, "selrep": selrep.reshape(NB, P),
        "jmask": jmask.reshape(NB, NT * K), "wk": wk, "kbias": kbias, "tmask": tmask, "bmask": np.repeat(np.eye(TB, dtype=np.float32), ROWS, 0),
        "ident": np.eye(P, dtype=np.float32), "cwT": v["L1_cond_c_weight"].T, "fside": everywhere(v["fside_S_0"]),
        "bbase": everywhere(cols(v["L1_ffn_b_base"])), "wgu": gu, "wdn": dn,
        "wconv": wconv.reshape(P, CB, P), "wbase": cols(rows(v["L1_ffn_W_base"].T)), "war": rows(a_r.T),
        "wlb": cols(v["L1_ffn_B_stack"].transpose(0, 2, 1).reshape(E1 * RANK, D)),
        "wr2": padded(rows(v["L2_ffn_router_weight"].T), NPAD), "rb2": everywhere(v["L2_ffn_router_bias"]),
        "eb2": np.tile(cols(v["L2_ffn_expert_bias"]), (2, 1)),
        "wr3": padded(rows(v["L3_ffn_gate_w"].T), NPAD),
        "wsg": cols(rows(v["L3_ffn_weight"].T)).reshape(P, S * D), "bias3": everywhere(cols(v["L3_ffn_bias"])),
        "inc3": four(cols(v["L3_ffn_in_channel_scale"])), "outc3": four(cols(v["L3_ffn_out_channel_scale"])),
    }
    nc = bacc.Bacc("TRN2", target_bir_lowering=False, num_devices=1)
    arrays, aps = {}, {}
    for name, a in host.items():
        a = np.ascontiguousarray(a)
        arrays["in_" + name] = a
        aps[name] = nc.dram_tensor("in_" + name, a.shape, mybir.dt.from_np(a.dtype), kind="ExternalInput").ap()
    out = nc.dram_tensor("out_x", (NB * ROWS, D), F32, kind="ExternalOutput").ap()
    build(nc, aps, out)
    r = launch(nc, [arrays], core_ids=[0])
    y = np.asarray(r.results[0]["out_x"])
    return np.ascontiguousarray(y.reshape(NB * ROWS, S, P).swapaxes(-1, -2)).reshape(NB, ROWS, D)
```

```python
from contextlib import ExitStack

import concourse.bass as bass
from concourse import mybir

F32 = mybir.dt.float32
F32R = mybir.dt.float32r
ALU = mybir.AluOpType
ACT = mybir.ActivationFunctionType
AX = mybir.AxisListType.X

P = 128
D = 512
S = D // P
ROWS = 32
NB = 64
TB = P // ROWS
NT = NB // TB
GT = 4
G = NT // GT
GB = GT * TB
TOK = GT * P
K = 8
HID = 128
FF = 1792
M = FF // P
E1, RANK, TOP1 = 8, 16, 2
LORA_SCALE = 32.0 / RANK
AR = E1 * RANK + E1
E2, TOP2 = 64, 8
E3 = 8
NPAD = 96
TAPS, PAD = 9, 4
MLPW = 2 * HID + K + 2
CB = 3
ds = bass.ds


def build(nc, A, out):
    ctx = ExitStack()
    with ctx:
        def sb(name, shape, dt=F32):
            return ctx.enter_context(nc.sbuf_tensor(name, shape, dt))

        def sem(name):
            return ctx.enter_context(nc.semaphore(name))

        def views(t, *widths):
            at, out = 0, []
            for w in widths:
                out.append(t[:, at:at + w])
                at += w
            return out

        x_all = sb("x_all", [P, NT, D])
        xs = sb("xs", [P, GT, D])
        cT = sb("cT", [P, S, TOK])
        c_hi = sb("c_hi", [P, S, TOK], F32R)
        c_lo = sb("c_lo", [P, S, TOK], F32R)
        silu = sb("silu", [P, 2, TOK])
        hff = sb("hff", [P, 2, TOK])
        h_hi = sb("h_hi", [P, 2, TOK], F32R)
        h_lo = sb("h_lo", [P, 2, TOK], F32R)
        agg = sb("agg", [P, 3, NT, ROWS])
        prod = sb("prod", [P, GT, K, ROWS])
        blk = sb("blk", [P, GT, P])
        bias_bc = sb("bias_bc", [P, TOK])
        pack_a = sb("pack_a", [P, 3 * MLPW + NB])
        w0, condT = views(pack_a, 3 * MLPW, NB)
        w0 = w0.rearrange("p (i n) -> p i n", i=3)
        pack_b = sb("pack_b", [NB, 3 * K + P + NT * K + ROWS])
        b2, selrep, jmask, fside = views(pack_b, 3 * K, P, NT * K, ROWS)
        pack_c = sb("pack_c", [P, 3 * K * ROWS + 3 * ROWS + TB + P + ROWS])
        wk, kbias, bmask, ident, cwT = views(pack_c, 3 * K * ROWS, 3 * ROWS, TB, P, ROWS)
        wk = wk.rearrange("p (i k o) -> p i k o", i=3, k=K)
        h1 = sb("h1", [P, 3, NB])
        h2 = sb("h2", [P, 3, NB])
        att = sb("att", [NB, 3, K])
        att_m = sb("att_m", [NB, 3, NT * K])
        att_bc = sb("att_bc", [P, 3, NT * K])
        attT = sb("attT", [P, 3, NB])
        btab = sb("btab", [NB, 4, ROWS])
        st0 = sb("st0", [NB, 2, 3])
        stg = sb("stg", [P, GB, P + 2])
        wconv = sb("wconv", [P, CB, P])
        scrap = sb("scrap", [P, 1])
        ones = sb("ones", [P, P])
        stat = sb("stat", [P, 4, GT])
        m8 = sb("m8", [P, GT, 8])
        t8 = sb("t8", [P, GT, 8])

        with ExitStack() as first:
            wl0 = first.enter_context(nc.sbuf_tensor("wl0", [P, M, 2 * S * P + D], F32R))
        lg = sb("lg", [P, GT, E2])
        ex = sb("ex", [P, GT, E2])
        rest = sb("rest", [P, GT, E2])
        war = sb("war", [P, S, AR])
        wbase = sb("wbase", [P, S, D])
        wlb = sb("wlb", [P, D])
        bbase = sb("bbase", [P, D])
        hm = sb("hm", [P, GT, P])
        hmT = sb("hmT", [P, TOK])
        wr2 = sb("wr2", [P, S, NPAD])
        wr3 = sb("wr3", [P, S, NPAD])
        rb2 = sb("rb2", [P, E2])
        eb2 = sb("eb2", [P, D])
        wsg = sb("wsg", [P, S, D])
        bias3 = sb("bias3", [P, D])
        inc3 = sb("inc3", [P, D])
        outc3 = sb("outc3", [P, D])
        t1 = sb("t1", [P, GT, D])
        osc = sb("osc", [P, GT, D])
        wcat = sb("wcat", [P, GT, P])
        rcat = sb("rcat", [P, GT, P])
        eb_hi = sb("eb_hi", [P, D], F32R)
        eb_lo = sb("eb_lo", [P, D], F32R)
        sgn = sb("sgn", [P, S, D], F32R)
        in_w = sb("in_w", [P, D], F32R)
        out_w = sb("out_w", [P, D], F32R)
        wT = sb("wT", [P, TOK], F32R)

        bias_dram = nc.dram_tensor("bias_dram", (NB, 4, ROWS), F32).ap()

        ps = ctx.enter_context(nc.psum_tensor("ps", [P, 8, 512], F32))

        def bank(i):
            return ps[:, i, :]

        terms = silu[:, 0]
        prod0 = hff[:].rearrange("p b (j k o) -> p (b j) k o", k=K, o=ROWS)

        s_pa, s_pb, s_pc = sem("s_pa"), sem("s_pb"), sem("s_pc")
        s_x = sem("s_x")
        s_w0 = [sem(f"s_w0_{m}") for m in range(M)]
        s_conv = sem("s_conv")
        s_l1w = sem("s_l1w")
        s_l23w = sem("s_l23w")
        s_pad = sem("s_pad")
        s_scr = sem("s_scr")
        s_mlp = sem("s_mlp")
        s_gelu = sem("s_gelu")
        s_att = sem("s_att")
        s_aexp = sem("s_aexp")
        s_abc = sem("s_abc")
        s_abcv = sem("s_abcv")
        s_aT = sem("s_aT")
        s_aTv = sem("s_aTv")
        s_bt, s_btv = sem("s_bt"), sem("s_btv")
        s_btd = sem("s_btd")
        s_agg = [sem(f"s_agg{i}") for i in range(3)]
        s_dv = sem("s_dv")
        s_pl = sem("s_pl")
        s_xs = [sem(f"s_xs{i}") for i in range(4)]
        s_bb = [sem(f"s_bb{i}") for i in range(4)]
        s_blk = [sem(f"s_blk{i}") for i in range(4)]
        s_cmm = [sem(f"s_cmm{i}") for i in range(4)]
        s_c = [sem(f"s_c{i}") for i in range(4)]
        s_acc = [sem(f"s_acc{i}") for i in range(4)]
        s_y = [sem(f"s_y{i}") for i in range(4)]
        s_terms, s_b0 = sem("s_terms"), sem("s_b0")
        s_mix0 = sem("s_mix0")
        s_chi = sem("s_chi")
        s_clo, s_clo_odd = sem("s_clo"), sem("s_clo_odd")
        s_gate, s_up = sem("s_gate"), sem("s_up")
        s_silu, s_h, s_hhi, s_hlo = sem("s_silu"), sem("s_h"), sem("s_hhi"), sem("s_hlo")
        s_ar, s_lg1, s_ex1, s_hm = sem("s_ar"), sem("s_lg1"), sem("s_ex1"), sem("s_hm")
        s_tr1, s_hmT, s_xb1 = sem("s_tr1"), sem("s_hmT"), sem("s_xb1")
        s_hi23, s_lo23 = sem("s_hi23"), sem("s_lo23")
        s_r2, s_lg2, s_ex2, s_wc = sem("s_r2"), sem("s_lg2"), sem("s_ex2"), sem("s_wc")
        s_ws, s_ct, s_t1, s_px = sem("s_ws"), sem("s_ct"), sem("s_t1"), sem("s_px")
        s_tr2, s_wT = sem("s_tr2"), sem("s_wT")
        s_r3, s_lg3, s_ex3, s_rc = sem("s_r3"), sem("s_lg3"), sem("s_ex3"), sem("s_rc")
        s_tr3, s_rT, s_in, s_os, s_osc = sem("s_tr3"), sem("s_rT"), sem("s_in"), sem("s_os"), sem("s_osc")
        s_xm, s_xhi, s_xlo = sem("s_xm"), sem("s_xhi"), sem("s_xlo")
        s_xb3, s_f3 = sem("s_xb3"), sem("s_f3")
        s_out = sem("s_out")

        block = ctx.enter_context(nc.Block())

        COND = {0: 0, 2: 1, 3: 2}
        CB4 = [4, 5, 6, 7]
        CBANKS = {(0, True): CB4, (0, False): CB4, (1, True): CB4, (1, False): CB4,
                  (2, True): [5, 6, 7, 5], (2, False): [5, 6, 7, 4],
                  (3, True): [5, 6, 7, 4], (3, False): CB4}
        ORDER2 = [3, 0, 1, 2]
        STG = 16 * S * TB

        @block.sync
        def _(sp):
            xd = A["x"].rearrange("(j p) n -> p j n", p=P)
            od = out.rearrange("(j p) n -> p j n", p=P)
            sp.dma_start(pack_a[:], A["pack_a"]).then_inc(s_pa, 16)
            sp.dma_start(pack_c[:], A["pack_c"]).then_inc(s_pc, 16)
            sp.dma_start(xs[:], xd[:, 0:GT, :]).then_inc(s_xs[0], 16)

            def bias(l, g):
                if l > 0 or g > 0:
                    before, done = (l, g * S) if g else (l - 1, G * S)
                    sp.wait_ge(s_c[before], done)
                src = bias_dram[g * GB:(g + 1) * GB, l, :].unsqueeze(0).broadcast_to([P, GB, ROWS])
                sp.dma_start(bias_bc[:].rearrange("p (b o) -> p b o", o=ROWS), src).then_inc(s_bb[l], 16)

            def regroup(g):
                sp.wait_ge(s_y[0], (g + 1) * GT)
                if g:
                    sp.wait_ge(s_cmm[1], g * GT)
                for s in range(S):
                    for b in range(TB):
                        src = x_all[b * ROWS:(b + 1) * ROWS, g * GT:(g + 1) * GT, s * P:(s + 1) * P]
                        dst = stg[s * ROWS:(s + 1) * ROWS, b:GB:TB, 1:P + 1]
                        sp.dma_start(dst, src).then_inc(s_xs[1], 16)

            def stage(l, g):
                before, done = (l, g * S) if g else ({2: 0, 3: 2}[l], G * S)
                sp.wait_ge(s_cmm[before], done)
                sp.wait_ge(s_y[l - 1], (g + 1) * GT)
                sp.dma_start(xs[:], x_all[:, g * GT:(g + 1) * GT, :]).then_inc(s_xs[l], 16)

            sp.wait_ge(s_btv, 2)
            sp.dma_start(bias_dram, btab[:]).then_inc(s_btd, 16)
            sp.wait_ge(s_btd, 16)
            sp.wait_ge(s_w0[M - 1], 16)
            sp.dma_start(x_all[:], xd).then_inc(s_x, 16)
            sp.dma_start(wconv[:], A["wconv"]).then_inc(s_conv, 16)
            for g in range(1, G):
                bias(0, g)
                sp.wait_ge(s_cmm[0], g * S)
                sp.dma_start(xs[:], xd[:, g * GT:(g + 1) * GT, :]).then_inc(s_xs[0], 16)
                if g == 1:
                    sp.wait_ge(s_pad, 1)
                    regroup(0)
            bias(1, 0)
            sp.wait_ge(s_up, G * M)
            for dst, src in ((war, "war"), (wbase, "wbase"), (bbase, "bbase"), (wlb, "wlb")):
                sp.dma_start(dst[:], A[src]).then_inc(s_l1w, 16)
            for dst, src in ((eb2, "eb2"), (inc3, "inc3"), (outc3, "outc3"), (wsg, "wsg"),
                             (wr2, "wr2"), (rb2, "rb2"), (wr3, "wr3"), (bias3, "bias3")):
                sp.dma_start(dst[:], A[src]).then_inc(s_l23w, 16)
            for g in range(1, G):
                regroup(g)
                bias(1, g)
            for l in (2, 3):
                for g in range(G):
                    stage(l, g)
                    bias(l, g)
            for g in range(G):
                for j in range(g * GT, (g + 1) * GT):
                    sp.wait_ge(s_y[3], j + 1)
                    sp.dma_start(od[:, j, :], x_all[:, j, :]).then_inc(s_out, 16)
            sp.wait_ge(s_out, 16 * NT)

        @block.gpsimd
        def _(pool):
            pool.memset(stg[:, :, 0:P + 2:P + 1], 0.0).then_inc(s_pad, 1)

            def weights(m0, m1):
                for m in range(m0, m1):
                    pool.dma_start(wl0[:, m, :], A["wl0"][m]).then_inc(s_w0[m], 16)

            chain = [0]

            def step(ins):
                chain[0] += 1
                ins.then_inc(s_pl, 1)
                pool.wait_ge(s_pl, chain[0])

            def mix(i, q):
                a = att_bc[:, i, q * GT * K:(q + 1) * GT * K].rearrange("p (j k) -> p j k", k=K)
                step(pool.tensor_tensor(prod[:], a.unsqueeze(3).broadcast_to([P, GT, K, ROWS]),
                                        wk[:, i].unsqueeze(1).broadcast_to([P, GT, K, ROWS]), ALU.mult))
                for n in (4, 2):
                    step(pool.tensor_tensor(prod[:, :, 0:n], prod[:, :, 0:n], prod[:, :, n:2 * n], ALU.add))
                pool.tensor_tensor(agg[:, i, q * GT:(q + 1) * GT], prod[:, :, 0], prod[:, :, 1],
                                   ALU.add).then_inc(s_agg[i], 1)
                pool.wait_ge(s_agg[i], q + 1)

            def split_c(g):
                for n, s in enumerate((1, 3)):
                    pool.wait_ge(s_chi, S * g + s + 1)
                    pool.tensor_tensor(c_lo[:, s], cT[:, s], c_hi[:, s].bitcast(F32), ALU.subtract).then_inc(s_clo_odd, 1)

            def block_diagonal(l, g):
                if not isinstance(g, int) or g > 0:
                    pool.wait_ge(s_cmm[l], g * S)
                elif l > 0:
                    pool.wait_ge(s_cmm[{2: 0, 3: 2}[l]], G * S)
                pool.tensor_tensor(blk[:].rearrange("p j (b o) -> p j b o", b=TB),
                                   agg[:, COND[l], ds(g * GT, GT)].unsqueeze(2).broadcast_to([P, GT, TB, ROWS]),
                                   bmask.unsqueeze(1).unsqueeze(3).broadcast_to([P, GT, TB, ROWS]),
                                   ALU.mult).then_inc(s_blk[l], 1)

            weights(0, 3)
            pool.wait_ge(s_pc, 16)
            pool.wait_ge(s_aTv, 1)
            pool.tensor_tensor(terms.rearrange("p (b o) -> p b o", o=ROWS),
                               attT[:, 0, 0:GB].unsqueeze(2).broadcast_to([P, GB, ROWS]),
                               kbias[:, 0:ROWS].unsqueeze(1).broadcast_to([P, GB, ROWS]), ALU.mult).then_inc(s_terms, 1)
            split_c(0)
            weights(3, M)
            pool.wait_ge(s_abcv, 2)
            for q in range(1, G):
                mix(0, q)
            for i in (1, 2):
                for q in range(G):
                    mix(i, q)
            with pool.Fori(1, G) as g:
                block_diagonal(0, g)
                split_c(g)
            block_diagonal(2, 0)

            def base_bias(g):
                pool.wait_ge(s_l1w, 64)
                pool.wait_ge(s_xs[1], STG * (g + 1))
                xg = x_all[:, ds(g * GT, GT), :]
                pool.tensor_tensor(xg, xg, bbase[:].unsqueeze(1).broadcast_to([P, GT, D]),
                                   ALU.add).then_inc(s_xb1, 1)

            base_bias(0)
            pool.wait_ge(s_l23w, 16 * 8)
            pool.wait_ge(s_hi23, 4)
            half = P // 2
            pool.wait_ge(s_xb1, 1)
            pool.tensor_tensor(eb_lo[:], eb2[:], eb_hi[:].bitcast(F32), ALU.subtract).then_inc(s_lo23, 1)
            pool.wait_ge(s_lo23, 1)
            for n, (w, src) in enumerate(((in_w, inc3), (out_w, outc3))):
                pool.tensor_tensor(w[half:P], src[half:P], w[half:P].bitcast(F32), ALU.subtract).then_inc(s_lo23, 1)
                pool.wait_ge(s_lo23, n + 2)
            with pool.Fori(1, G) as g:
                base_bias(g)

            def add_scaled(g):
                pool.wait_ge(s_xs[2], (g + 1) * 16)
                for n, j in enumerate(ORDER2):
                    pool.wait_ge(s_t1, g * GT + n + 1)
                    xg = x_all[:, ds(g * GT + j, 1), :]
                    pool.tensor_tensor(xg, xg, t1[:, j:j + 1, :], ALU.add).then_inc(s_px, 1)

            with pool.Fori(1, G) as g:
                block_diagonal(2, g)
                add_scaled(g - 1)
            block_diagonal(3, 0)
            add_scaled(G - 1)

            def bias_3(g):
                pool.wait_ge(s_xs[3], 16 * (g + 1))
                xg = x_all[:, ds(g * GT, GT), :]
                pool.tensor_tensor(xg, xg, bias3[:].unsqueeze(1).broadcast_to([P, GT, D]), ALU.add).then_inc(s_xb3, 1)

            def finish_3(g):
                pool.wait_ge(s_xb3, g + 1)
                for j in range(GT):
                    pool.wait_ge(s_f3, g * GT + j + 1)
                    xg = x_all[:, ds(g * GT + j, 1), :]
                    pool.tensor_tensor(xg, xg, t1[:, j:j + 1, :], ALU.add).then_inc(s_y[3], 1)

            bias_3(0)
            block_diagonal(3, 1)
            with pool.Fori(1, G - 1) as g:
                bias_3(g)
                block_diagonal(3, g + 1)
                finish_3(g - 1)
            bias_3(G - 1)
            finish_3(G - 2)
            finish_3(G - 1)

        @block.tensor
        def _(pe):
            def mm(o, l, r, start=True, stop=True):
                return pe.matmul(o, l, r, start=start, stop=stop)

            def cols(j):
                return slice(j * P, (j + 1) * P)

            pe.wait_ge(s_pa, 16)
            for i in range(3):
                mm(bank(0)[:, i * NB:(i + 1) * NB], w0[:, i, 0:HID], condT).then_inc(s_mlp, 1)
            pe.wait_ge(s_gelu, 3)
            for i in range(3):
                mm(bank(1)[:, i * NB:(i + 1) * NB], w0[:, i, HID:2 * HID], h1[:, i]).then_inc(s_mlp, 1)
            pe.wait_ge(s_gelu, 6)
            for i in range(3):
                mm(bank(2)[0:NB, i * K:(i + 1) * K], h2[:, i], w0[:, i, 2 * HID:2 * HID + K]).then_inc(s_mlp, 1)
            pe.wait_ge(s_att, 7)
            mm(bank(3)[:, 0:NT * K], selrep, att_m[:, 0]).then_inc(s_abc, 1)
            pe.wait_ge(s_pc, 16)
            pe.transpose(bank(0)[:, 0:NB], att_m[:, 0], ident[0:NB, 0:NB]).then_inc(s_aT, 1)
            pe.wait_ge(s_att, 9)
            mm(bank(2)[:, 0:2 * NT * K], selrep, att_m[:, 1:3].rearrange("b i n -> b (i n)")).then_inc(s_abc, 1)
            for i in (1, 2):
                ins = pe.transpose(bank(1)[:, (i - 1) * NB:i * NB], att_m[:, i], ident[0:NB, 0:NB])
            ins.then_inc(s_aT, 1)
            pe.wait_ge(s_terms, 1)
            mm(bank(0), ones[:], terms).then_inc(s_b0, 1)
            pe.wait_ge(s_aTv, 2)
            for l, i in COND.items():
                mm(bank(1)[0:NB, l * ROWS:(l + 1) * ROWS], attT[:, i], kbias[:, i * ROWS:(i + 1) * ROWS])
            mm(bank(1)[0:NB, ROWS:2 * ROWS], condT, cwT).then_inc(s_bt, 1)

            def nothing():
                pass

            def cond_chunk(l, g, s, b):
                for j in range(GT):
                    ins = mm(bank(b)[:, cols(j)], xs[:, j, cols(s)], blk[:, j])
                ins.then_inc(s_cmm[l], 1)

            def cond(l, g, first, before):
                pe.wait_ge(s_xs[l], 16 * (g + 1))
                pe.wait_ge(s_blk[l], g + 1)
                for s, b in enumerate(CBANKS[l, first]):
                    before[s]()
                    cond_chunk(l, g, s, b)

            def gate_up(g, m):
                n = g * M + m
                pe.wait_ge(s_w0[m], 16)
                if m >= 2:
                    pe.wait_ge(s_h, n - 1)
                b = 4 + 2 * (m % 2)
                for u, done in ((0, s_gate), (1, s_up)):
                    for s in range(S):
                        if m == 0 and u == 0:
                            pe.wait_ge(s_clo_odd if s % 2 else s_clo, 2 * g + s // 2 + 1)
                        w = wl0[:, m, cols(u * S + s)]
                        for c in (c_hi, c_lo):
                            ins = mm(bank(b + u), w, c[:, s], start=s == 0 and c is c_hi, stop=s == S - 1 and c is c_lo)
                    ins.then_inc(done, 1)

            def down(g, m):
                pe.wait_ge(s_hlo, g * M + m + 1)
                w = wl0[:, m, 2 * S * P:2 * S * P + D]
                for j in range(GT):
                    mm(bank(j), h_hi[:, m % 2, cols(j)], w, start=m == 0, stop=False)
                    ins = mm(bank(j), h_lo[:, m % 2, cols(j)], w, start=False, stop=m == M - 1)
                    if m == M - 1:
                        ins.then_inc(s_acc[0], 1)

            def conv(g, j):
                if j == 0:
                    pe.wait_ge(s_xs[1], STG * (g + 1))
                for b in range(TB):
                    for c in range(CB):
                        ins = mm(bank(4 + j)[:, cols(b)], stg[:, j * TB + b, c:c + P], wconv[:, c],
                                 start=c == 0, stop=c == CB - 1)
                ins.then_inc(s_cmm[1], 1)

            def layer0(g, more):
                for m in range(M):
                    gate_up(g, m)
                    if m >= 1:
                        down(g, m - 1)
                pe.wait_ge(s_h, g * M + M - 1)
                if more:
                    cond(0, g + 1, False, [nothing, nothing, lambda: pe.wait_ge(s_h, g * M + M), nothing])
                else:
                    pe.wait_ge(s_conv, 16)
                    for j in range(GT):
                        if j == 2:
                            pe.wait_ge(s_h, g * M + M)
                        conv(0, j)
                down(g, M - 1)

            cond(0, 0, True, [nothing] * 4)
            with pe.Fori(0, G - 1) as g:
                layer0(g, True)
            layer0(G - 1, False)

            def lora_a_router(g):
                pe.wait_ge(s_l1w, 64)
                pe.wait_ge(s_c[1], GT * g + GT)
                for j in range(GT):
                    for s in range(S):
                        ins = mm(bank(4 + j)[:, 0:AR], cT[:, s, cols(j)], war[:, s], s == 0, s == S - 1)
                ins.then_inc(s_ar, 1)

            def base(g):
                for j in range(GT):
                    for s in range(S):
                        mm(bank(j), cT[:, s, cols(j)], wbase[:, s], s == 0, False)

            def turn_hm(g):
                for j in range(GT):
                    ins = pe.transpose(bank(4)[:, cols(j)], hm[:, j], ident)
                ins.then_inc(s_tr1, 1)

            def lora_b(g):
                pe.wait_ge(s_hmT, g + 1)
                for j in range(GT):
                    mm(bank(j), hmT[:, cols(j)], wlb[:], False, True).then_inc(s_acc[1], 1)

            def layer1(g, more):
                base(g)
                pe.wait_ge(s_hm, g + 1)
                if more:
                    for j in range(GT - 1):
                        conv(g + 1, j)
                    pe.wait_ge(s_c[1], GT * (g + 1) + 1)
                    turn_hm(g)
                    conv(g + 1, GT - 1)
                    lora_b(g)
                    lora_a_router(g + 1)
                else:
                    cond(2, 0, True, [nothing, nothing, nothing, lambda: (turn_hm(g), pe.wait_ge(s_c[2], 1))])
                    lora_b(g)
                    pe.wait_ge(s_lo23, 3)
                    pe.wait_ge(s_l23w, 16 * 8)
                    router2(0)
                pe.wait_ge(s_y[1], GT * (g + 1))

            def router2(g):
                pe.wait_ge(s_c[2], S * (g + 1))
                for j in range(GT):
                    for s in range(S):
                        ins = mm(bank(4)[:, j * P:j * P + NPAD], cT[:, s, cols(j)], wr2[:, s], s == 0, s == S - 1)
                ins.then_inc(s_r2, 1)

            def layer2(g, more):
                for j in ORDER2:
                    for s in range(S):
                        ins = pe.transpose(bank(j)[:, cols(s)], cT[:, s, cols(j)], ident)
                    ins.then_inc(s_ct, 1)
                free = [nothing, nothing, nothing, lambda: pe.wait_ge(s_lg2, g + 1)]
                if more:
                    cond(2, g + 1, False, free)
                else:
                    cond(3, 0, True, free)
                pe.wait_ge(s_wc, g + 1)
                pe.wait_ge(s_t1, GT * g + 1)
                for j in range(GT):
                    ins = pe.transpose(bank(3)[:, cols(j)], wcat[:, j], ident)
                ins.then_inc(s_tr2, 1)
                pe.wait_ge(s_wT, g + 1)
                for n, j in enumerate(ORDER2):
                    pe.wait_ge(s_t1, GT * g + n + 1)
                    mm(bank(j), wT[:, cols(j)], eb_hi[:], True, False)
                    mm(bank(j), wT[:, cols(j)], eb_lo[:], False, True).then_inc(s_acc[2], 1)
                if more:
                    router2(g + 1)
                else:
                    pe.wait_ge(s_hi23, 4)
                    router3(0)
                pe.wait_ge(s_y[2], GT * (g + 1))

            def router3(g):
                pe.wait_ge(s_c[3], S * (g + 1))
                for j in range(GT):
                    for s in range(S):
                        ins = mm(bank(4)[:, j * P:j * P + NPAD], cT[:, s, cols(j)], wr3[:, s], s == 0, s == S - 1)
                ins.then_inc(s_r3, 1)

            def sign_product(g, js):
                pe.wait_ge(s_xlo, S * (g + 1))
                for j in js:
                    pe.wait_ge(s_osc, GT * g + j + 1)
                    for s in range(S):
                        mm(bank(j), c_hi[:, s, cols(j)], sgn[:, s], s == 0, False)
                        ins = mm(bank(j), c_lo[:, s, cols(j)], sgn[:, s], False, s == S - 1)
                    ins.then_inc(s_acc[3], 1)

            def scales(g, first):
                pe.wait_ge(s_rc, g + 1)
                for j in range(GT):
                    ins = pe.transpose(bank(5)[:, cols(j)], rcat[:, j], ident)
                ins.then_inc(s_tr3, 1)
                pe.wait_ge(s_rT, g + 1)
                for s in range(S):
                    mm(bank(4 + s), in_w[:, cols(s)], wT[:]).then_inc(s_in, 1)
                for j in range(GT):
                    if not first:
                        pe.wait_ge(s_f3, GT * (g - 1) + j + 1)
                    mm(bank(j), wT[:, cols(j)], out_w[:]).then_inc(s_os, 1)

            def cond3(g):
                cond(3, g, False, [(lambda s=s: pe.wait_ge(s_xm, S * (g - 1) + s + 1)) for s in range(S)])

            lora_a_router(0)
            pe.wait_ge(s_y[0], G * GT)
            with pe.Fori(0, G - 1) as g:
                layer1(g, True)
            layer1(G - 1, False)
            with pe.Fori(0, G - 1) as g:
                layer2(g, True)
            layer2(G - 1, False)
            scales(0, True)
            cond3(1)

            def layer3(g, more):
                sign_product(g, range(0, 2))
                router3(g + 1)
                sign_product(g, range(2, GT))
                scales(g + 1, False)
                if more:
                    cond3(g + 2)

            with pe.Fori(0, G - 2) as g:
                layer3(g, True)
            layer3(G - 2, False)
            sign_product(G - 1, range(GT))

        @block.scalar
        def _(act):
            def copy(o, i):
                return act.activation(o, i, ACT.Copy)

            act.dma_start(pack_b[:], A["pack_b"]).then_inc(s_pb, 16)
            act.wait_ge(s_scr, 1)
            act.activation(scrap[:], scrap[:], ACT.Gelu)
            act.wait_ge(s_pa, 16)
            for n, dst in enumerate((h1, h2)):
                act.wait_ge(s_mlp, 3 * n + 3)
                for i in range(3):
                    at = 2 * HID + K + n
                    act.activation(dst[:, i], bank(n)[:, i * NB:(i + 1) * NB], ACT.Gelu,
                                   bias=w0[:, i, at:at + 1]).then_inc(s_gelu, 1)
            act.wait_ge(s_att, 3)
            act.activation(att[:], att[:], ACT.Exp).then_inc(s_aexp, 1)
            act.wait_ge(s_aT, 1)
            copy(attT[:, 0], bank(0)[:, 0:NB]).then_inc(s_aTv, 1)
            act.wait_ge(s_aT, 2)
            copy(attT[:, 1:3].rearrange("p i n -> p (i n)"), bank(1)[:, 0:2 * NB]).then_inc(s_aTv, 1)
            act.activation(scrap[:], scrap[:], ACT.Silu)
            act.wait_ge(s_b0, 1)
            copy(bias_bc[:], bank(0)).then_inc(s_bb[0], 16)
            copy(att_bc[:, 1:3].rearrange("p i n -> p (i n)"), bank(2)[:, 0:2 * NT * K]).then_inc(s_abcv, 1)
            act.wait_ge(s_mix0, 1)
            copy(att_bc[:, 0], bank(3)[:, 0:NT * K]).then_inc(s_abcv, 1)
            act.wait_ge(s_bt, 1)
            copy(btab[:].rearrange("b l o -> b (l o)"), bank(1)[0:NB, 0:4 * ROWS]).then_inc(s_btv, 1)

            def split_c(g):
                for s in range(S):
                    act.wait_ge(s_c[0], S * g + s + 1)
                    copy(c_hi[:, s], cT[:, s]).then_inc(s_chi, 1)

            def layer0(g, more):
                for m in range(M):
                    n = g * M + m
                    act.wait_ge(s_gate, n + 1)
                    act.activation(silu[:, m % 2], bank(4 + 2 * (m % 2)), ACT.Silu).then_inc(s_silu, 1)
                    act.wait_ge(s_h, n + 1)
                    copy(h_hi[:, m % 2], hff[:, m % 2]).then_inc(s_hhi, 1)
                if more:
                    split_c(g + 1)

            split_c(0)
            with act.Fori(0, G - 1) as g:
                layer0(g, True)
            layer0(G - 1, False)

            act.wait_ge(s_l23w, 16 * 8)
            act.wait_ge(s_acc[0], G * GT)
            for dst, src in ((eb_hi, eb2), (in_w, inc3), (out_w, outc3)):
                copy(dst[:], src[:]).then_inc(s_hi23, 1)
            act.activation(sgn[:], wsg[:], ACT.Sign).then_inc(s_hi23, 1)

            def exp(s_in, s_done, g, width):
                act.wait_ge(s_in, g + 1)
                act.activation(ex[:, :, 0:width], lg[:, :, 0:width], ACT.Exp).then_inc(s_done, 1)

            with act.Fori(0, G) as g:
                exp(s_lg1, s_ex1, g, E1)
                act.wait_ge(s_tr1, g + 1)
                copy(hmT[:], bank(4)).then_inc(s_hmT, 1)

            def scaled(g, j, n):
                act.wait_ge(s_ct, GT * g + n + 1)
                act.activation(t1[:, j], bank(j), ACT.Copy, scale=stat[:, 3, j:j + 1]).then_inc(s_t1, 1)

            def layer2(g, more):
                exp(s_lg2, s_ex2, g, E2)
                act.wait_ge(s_ws, g + 1)
                scaled(g, ORDER2[0], 0)
                scaled(g, ORDER2[1], 1)
                act.wait_ge(s_tr2, g + 1)
                copy(wT[:], bank(3)).then_inc(s_wT, 1)
                scaled(g, ORDER2[2], 2)
                scaled(g, ORDER2[3], 3)
                if more:
                    act.wait_ge(s_px, GT * (g + 1))

            with act.Fori(0, G - 1) as g:
                layer2(g, True)
            layer2(G - 1, False)

            def layer3(g):
                exp(s_lg3, s_ex3, g, E3)
                act.wait_ge(s_tr3, g + 1)
                copy(wT[:], bank(5)).then_inc(s_rT, 1)
                for n in range(S):
                    act.wait_ge(s_os, GT * g + n + 1)
                    copy(osc[:, n], bank(n)).then_inc(s_osc, 1)
                    act.wait_ge(s_xm, S * g + n + 1)
                    copy(c_hi[:, n], cT[:, n]).then_inc(s_xhi, 1)

            with act.Fori(0, G) as g:
                layer3(g)

        @block.vector
        def _(dve):
            def tt(o, a, b, op):
                return dve.tensor_tensor(o, a, b, op)

            dve.memset(scrap[:], 0.0).then_inc(s_scr, 1)
            dve.memset(ones[:], 1.0).then_inc(s_scr, 1)
            flat = att[:].rearrange("b i k -> b (i k)")
            dve.wait_ge(s_pb, 16)
            dve.wait_ge(s_mlp, 9)
            tt(flat, bank(2)[0:NB, 0:3 * K], b2, ALU.add).then_inc(s_att, 1)
            dve.wait_ge(s_att, 1)
            dve.tensor_reduce(st0[:, 0], att[:], AX, ALU.max).then_inc(s_att, 1)
            dve.wait_ge(s_att, 2)
            tt(att[:], att[:], st0[:, 0].unsqueeze(2).broadcast_to([NB, 3, K]), ALU.subtract).then_inc(s_att, 1)
            dve.wait_ge(s_aexp, 1)
            dve.tensor_reduce(st0[:, 0], att[:], AX, ALU.add).then_inc(s_att, 1)
            dve.wait_ge(s_att, 4)
            dve.reciprocal(st0[:, 1], st0[:, 0]).then_inc(s_att, 1)
            dve.wait_ge(s_att, 5)
            tt(att[:], att[:], st0[:, 1].unsqueeze(2).broadcast_to([NB, 3, K]), ALU.mult).then_inc(s_att, 1)
            dve.wait_ge(s_att, 6)
            for i in range(3):
                tt(att_m[:, i].rearrange("b (j k) -> b j k", k=K), jmask.rearrange("b (j k) -> b j k", k=K),
                   att[:, i].unsqueeze(1).broadcast_to([NB, NT, K]), ALU.mult).then_inc(s_att, 1)
            dve.wait_ge(s_pc, 16)
            dve.wait_ge(s_abc, 1)
            a = bank(3)[:, 0:GT * K].rearrange("p (j k) -> p j k", k=K)
            tt(prod0, a.unsqueeze(3).broadcast_to([P, GT, K, ROWS]),
               wk[:, 0].unsqueeze(1).broadcast_to([P, GT, K, ROWS]), ALU.mult).then_inc(s_mix0, 1)
            dve.wait_ge(s_mix0, 1)
            dve.tensor_reduce(agg[:, 0, 0:GT], prod0.rearrange("p j k o -> p j o k"), AX, ALU.add).then_inc(s_agg[0], 1)
            dve.wait_ge(s_agg[0], 1)
            tt(blk[:].rearrange("p j (b o) -> p j b o", b=TB),
               agg[:, 0, 0:GT].unsqueeze(2).broadcast_to([P, GT, TB, ROWS]),
               bmask.unsqueeze(1).unsqueeze(3).broadcast_to([P, GT, TB, ROWS]), ALU.mult).then_inc(s_blk[0], 1)

            def cond(l, g, first, split=None):
                dve.wait_ge(s_bb[l], 16 * (g + 1))
                banks = CBANKS[l, first]
                for s in range(S + 1):
                    if s < S:
                        dve.wait_ge(s_cmm[l], S * g + s + 1)
                        tt(cT[:, s], bank(banks[s]), bias_bc[:], ALU.add).then_inc(s_c[l], 1)
                    if split and s >= 1:
                        split(g, s - 1)

            def cond1(g):
                dve.wait_ge(s_bb[1], 16 * (g + 1))
                v = bias_bc[:].rearrange("p (b o) -> p b o", o=ROWS)
                for j in range(GT):
                    dve.wait_ge(s_cmm[1], GT * g + j + 1)
                    o = cT[:, :, j * P:(j + 1) * P].rearrange("p s (b o) -> p b s o", o=ROWS)
                    tt(o, bank(4 + j).rearrange("p (b s o) -> p b s o", b=TB, s=S),
                       v[:, j * TB:(j + 1) * TB].unsqueeze(2).broadcast_to([P, TB, S, ROWS]), ALU.add).then_inc(s_c[1], 1)

            def residual(l, g):
                for j in range(GT):
                    dve.wait_ge(s_acc[l], GT * g + j + 1)
                    xt = x_all[:, ds(g * GT + j, 1), :]
                    tt(xt, xt, bank(j).unsqueeze(1), ALU.add).then_inc(s_y[l], 1)

            def split_c(g, s):
                if s % 2:
                    return
                dve.wait_ge(s_chi, S * g + s + 1)
                tt(c_lo[:, s], cT[:, s], c_hi[:, s].bitcast(F32), ALU.subtract).then_inc(s_clo, 1)

            def layer0(g, more):
                for m in range(M):
                    n = g * M + m
                    dve.wait_ge(s_silu, n + 1)
                    dve.wait_ge(s_up, n + 1)
                    tt(hff[:, m % 2], silu[:, m % 2], bank(5 + 2 * (m % 2)), ALU.mult).then_inc(s_h, 1)
                    dve.wait_ge(s_hhi, n + 1)
                    tt(h_lo[:, m % 2], hff[:, m % 2], h_hi[:, m % 2].bitcast(F32), ALU.subtract).then_inc(s_hlo, 1)
                if more:
                    cond(0, g + 1, False, split_c)
                else:
                    cond1(0)
                dve.wait_ge(s_x, 16)
                residual(0, g)

            cond(0, 0, True, split_c)
            dve.wait_ge(s_btv, 1)
            tt(btab[:, 1], btab[:, 1], fside, ALU.add).then_inc(s_btv, 1)
            with dve.Fori(0, G - 1) as g:
                layer0(g, True)
            layer0(G - 1, False)

            def bc(v, n):
                return v.unsqueeze(2).broadcast_to([P, GT, n])

            def alone():
                dve.memset(scrap[:], 0.0)

            def linker(base, per, g):
                n = [0]

                def link(ins, apart=False):
                    n[0] += 1
                    ins.then_inc(s_dv, 1)
                    dve.wait_ge(s_dv, base + per * g + n[0])
                    if apart:
                        alone()
                link.count = n
                return link

            PER1, PER2, PER3 = 9, 8, 6
            base2 = PER1 * G
            base3 = base2 + PER2 * G

            def route1(g):
                link = linker(0, PER1, g)
                e, c = ex[:, :, 0:E1], lg[:, :, 0:E1]
                head = ps[:, 4:8, E1 * RANK:AR]
                dve.wait_ge(s_ar, g + 1)
                link(dve.tensor_reduce(stat[:, 0], head, AX, ALU.max))
                tt(c, head, bc(stat[:, 0], E1), ALU.subtract).then_inc(s_lg1, 1)
                dve.wait_ge(s_ex1, g + 1)
                alone()
                for j in range(GT):
                    ins = dve.max(m8[:, j], ex[:, j, 0:E1])
                link(ins)
                link(dve.tensor_copy(t8[:, :, 0:TOP1], m8[:, :, 0:TOP1]), True)
                for j in range(GT):
                    ins = dve.match_replace(rest[:, j, 0:E1], t8[:, j], ex[:, j, 0:E1], 0.0)
                link(ins)
                link(tt(stat[:, 1], m8[:, :, 0], m8[:, :, 1], ALU.add))
                link(tt(c, e, rest[:, :, 0:E1], ALU.subtract))
                link(dve.reciprocal(stat[:, 2], stat[:, 1]))
                link(dve.tensor_scalar(stat[:, 2], stat[:, 2], LORA_SCALE, None, ALU.mult))
                link(tt(c, c, bc(stat[:, 2], E1), ALU.mult))
                assert link.count[0] == PER1
                h = ps[:, 4:8, 0:E1 * RANK].rearrange("p j (e r) -> p j e r", r=RANK)
                tt(hm[:].rearrange("p j (e r) -> p j e r", r=RANK), h,
                   c.unsqueeze(3).broadcast_to([P, GT, E1, RANK]), ALU.mult).then_inc(s_hm, 1)

            dve.memset(t8[:], -1.0).then_inc(s_scr, 1)
            dve.wait_ge(s_scr, 3)
            with dve.Fori(0, G - 1) as g:
                route1(g)
                cond1(g + 1)
                dve.wait_ge(s_xb1, g + 1)
                residual(1, g)
            route1(G - 1)
            cond(2, 0, True)
            dve.wait_ge(s_xb1, G)
            residual(1, G - 1)

            def route2(g):
                link = linker(base2, PER2, g)
                dve.wait_ge(s_r2, g + 1)
                lt = bank(4).rearrange("p (j e) -> p j e", j=GT)[:, :, 0:E2]
                link(tt(lg[:], lt, rb2[:].unsqueeze(1).broadcast_to([P, GT, E2]), ALU.add))
                link(dve.tensor_reduce(stat[:, 0], lg[:], AX, ALU.max))
                tt(lg[:], lg[:], bc(stat[:, 0], E2), ALU.subtract).then_inc(s_lg2, 1)
                dve.wait_ge(s_ex2, g + 1)
                alone()
                for j in range(GT):
                    ins = dve.max(m8[:, j], ex[:, j])
                link(ins)
                link(dve.tensor_reduce(stat[:, 1], ex[:], AX, ALU.add))
                dve.reciprocal(stat[:, 2], stat[:, 1])
                link(dve.tensor_reduce(stat[:, 0], m8[:], AX, ALU.add))
                tt(stat[:, 3], stat[:, 0], stat[:, 2], ALU.mult).then_inc(s_ws, 1)
                for j in range(GT):
                    ins = dve.match_replace(rest[:, j], m8[:, j], ex[:, j], 0.0)
                link(ins)
                link(tt(lg[:], ex[:], rest[:], ALU.subtract))
                link(dve.tensor_copy(wcat[:, :, 0:E2].bitcast(F32R), lg[:]))
                tt(wcat[:, :, E2:2 * E2], lg[:], wcat[:, :, 0:E2], ALU.subtract).then_inc(s_wc, 1)

            def final2(g):
                for n, j in enumerate(ORDER2):
                    dve.wait_ge(s_acc[2], GT * g + n + 1)
                    dve.wait_ge(s_px, GT * g + n + 1)
                    xt = x_all[:, ds(g * GT + j, 1), :]
                    dve.scalar_tensor_tensor(xt, bank(j).unsqueeze(1), stat[:, 2, j:j + 1], xt, ALU.mult,
                                             ALU.add).then_inc(s_y[2], 1)

            with dve.Fori(0, G - 1) as g:
                route2(g)
                cond(2, g + 1, False)
                final2(g)
            route2(G - 1)
            dve.memset(rcat[:], 0.0)
            cond(3, 0, True)
            final2(G - 1)

            def route3(g):
                link = linker(base3, PER3, g)
                dve.wait_ge(s_r3, g + 1)
                lt = bank(4).rearrange("p (j e) -> p j e", j=GT)[:, :, 0:E3]
                e = ex[:, :, 0:E3]
                link(dve.tensor_reduce(stat[:, 0], lt, AX, ALU.max))
                tt(lg[:, :, 0:E3], lt, bc(stat[:, 0], E3), ALU.subtract).then_inc(s_lg3, 1)
                dve.wait_ge(s_ex3, g + 1)
                link(dve.tensor_reduce(stat[:, 1], e, AX, ALU.add))
                link(dve.reciprocal(stat[:, 2], stat[:, 1]))
                link(tt(e, e, bc(stat[:, 2], E3), ALU.mult))
                r4 = rcat[:].rearrange("p j (q k) -> p j q k", q=4)
                for q in (0, 2):
                    ins = dve.tensor_copy(r4[:, :, q, 0:E3].bitcast(F32R), e)
                link(ins)
                link(tt(r4[:, :, 1, 0:E3], e, r4[:, :, 0, 0:E3], ALU.subtract))
                assert link.count[0] == PER3
                tt(r4[:, :, 3, 0:E3], e, r4[:, :, 0, 0:E3], ALU.subtract).then_inc(s_rc, 1)

            def scale_in(g):
                for s in range(S + 1):
                    if s < S:
                        dve.wait_ge(s_in, S * g + s + 1)
                        tt(cT[:, s], cT[:, s], bank(4 + s), ALU.mult).then_inc(s_xm, 1)
                    if s >= 1:
                        dve.wait_ge(s_xhi, S * g + s)
                        tt(c_lo[:, s - 1], cT[:, s - 1], c_hi[:, s - 1].bitcast(F32), ALU.subtract).then_inc(s_xlo, 1)

            def scale_out(g, js):
                for j in js:
                    dve.wait_ge(s_acc[3], GT * g + j + 1)
                    tt(t1[:, j], osc[:, j], bank(j), ALU.mult).then_inc(s_f3, 1)

            def layer3(g, more):
                scale_out(g, range(0, 2))
                route3(g + 1)
                scale_out(g, range(2, GT))
                scale_in(g + 1)
                if more:
                    dve.wait_ge(s_xlo, S * (g + 2))
                    cond(3, g + 2, False)
                dve.wait_ge(s_y[3], GT * (g + 1))

            route3(0)
            scale_in(0)
            dve.wait_ge(s_xlo, S)
            cond(3, 1, False)
            with dve.Fori(0, G - 2) as g:
                layer3(g, True)
            layer3(G - 2, False)
            scale_out(G - 1, range(GT))


def kernel(**inputs):
    import numpy as np
    import concourse.bacc as bacc
    from concourse.bass_utils import run_bass_kernel_spmd as launch

    v = {n: np.asarray(a) for n, a in inputs.items()}

    def cols(a):
        return a.reshape(*a.shape[:-1], P, S).swapaxes(-1, -2).reshape(a.shape)

    def rows(a):
        return a.reshape(P, S, a.shape[-1])

    def everywhere(a):
        return np.broadcast_to(a, (P, *a.shape))

    conds = ("L0_cond_", "L2_cond_", "L3_cond_")

    def padded(a, n):
        o = np.zeros((*a.shape[:-1], n), a.dtype)
        o[..., :a.shape[-1]] = a
        return o

    mlp = np.stack([np.concatenate([v[c + "W0"], v[c + "W1"], v[c + "W2"], v[c + "b0"][:, None],
                                    v[c + "b1"][:, None]], 1) for c in conds], 1)
    b2 = np.broadcast_to(np.concatenate([v[c + "b2"] for c in conds]), (NB, 3 * K))
    wk = np.stack([np.tile(v[c + "weight"][..., 0].transpose(2, 0, 1), (TB, 1, 1)) for c in conds], 1)
    kbias = np.stack([np.tile(v[c + "bias_k"], (NT, 1)) for c in conds], 1)
    bmask = np.repeat(np.eye(TB, dtype=np.float32), ROWS, 0)
    selrep = np.zeros((NB, TB, ROWS), np.float32)
    selrep[np.arange(NB), np.arange(NB) % TB] = 1
    jmask = np.zeros((NB, NT, K), np.float32)
    jmask[np.arange(NB), np.arange(NB) // TB] = 1
    cw = v["L1_cond_weight"]
    wconv = np.zeros((S, ROWS, CB, S, ROWS), np.float32)
    ig = cw.shape[1]
    for r in range(S):
        for tap in range(TAPS):
            at = r + tap - PAD + S
            for o in range(ROWS):
                i0 = o // ig * ig
                wconv[at % S, i0:i0 + ig, at // S, r, o] = cw[o, :, tap]

    def four(a):
        o = np.zeros((4, P // 4, a.shape[1]), a.dtype)
        o[:, :a.shape[0]] = a
        return o.reshape(P, -1)

    gu = np.stack([v["L0_ffn_W_gate"], v["L0_ffn_W_up"]])
    gu = gu.reshape(2, M, P, P, S).transpose(1, 3, 0, 4, 2).reshape(M, P, 2 * S * P)
    dn = cols(np.ascontiguousarray(v["L0_ffn_W_down"].T)).reshape(M, P, D)

    def beside(*parts):
        return np.concatenate([a.reshape(a.shape[0], -1) for a in parts], 1)

    a_r = np.concatenate([v["L1_ffn_A_stack"].reshape(E1 * RANK, D), v["L1_ffn_W_router"]])
    host = {
        "x": cols(v["x"].reshape(NB * ROWS, D)),
        "pack_a": beside(mlp, v["cond_128"].T),
        "pack_b": beside(b2, selrep, jmask, np.broadcast_to(v["fside_S_0"], (NB, ROWS))),
        "pack_c": beside(wk, kbias, bmask, np.eye(P, dtype=np.float32), v["L1_cond_c_weight"].T),
        "bbase": everywhere(cols(v["L1_ffn_b_base"])), "wl0": np.concatenate([gu, dn], 2),
        "wconv": wconv.reshape(P, CB, P), "wbase": cols(rows(v["L1_ffn_W_base"].T)), "war": rows(a_r.T),
        "wlb": cols(v["L1_ffn_B_stack"].transpose(0, 2, 1).reshape(E1 * RANK, D)),
        "wr2": padded(rows(v["L2_ffn_router_weight"].T), NPAD), "rb2": everywhere(v["L2_ffn_router_bias"]),
        "eb2": np.tile(cols(v["L2_ffn_expert_bias"]), (2, 1)),
        "wr3": padded(rows(v["L3_ffn_gate_w"].T), NPAD),
        "wsg": cols(rows(v["L3_ffn_weight"].T)), "bias3": everywhere(cols(v["L3_ffn_bias"])),
        "inc3": four(cols(v["L3_ffn_in_channel_scale"])), "outc3": four(cols(v["L3_ffn_out_channel_scale"])),
    }
    nc = bacc.Bacc("TRN2", target_bir_lowering=False, num_devices=1)
    arrays, aps = {}, {}
    for name, a in host.items():
        a = np.ascontiguousarray(a)
        arrays["in_" + name] = a
        aps[name] = nc.dram_tensor("in_" + name, a.shape, mybir.dt.from_np(a.dtype), kind="ExternalInput").ap()
    out = nc.dram_tensor("out_x", (NB * ROWS, D), F32, kind="ExternalOutput").ap()
    build(nc, aps, out)
    r = launch(nc, [arrays], core_ids=[0])
    y = np.asarray(r.results[0]["out_x"])
    return np.ascontiguousarray(y.reshape(NB * ROWS, S, P).swapaxes(-1, -2)).reshape(NB, ROWS, D)
```

```python
from contextlib import ExitStack

import concourse.bass as bass
from concourse import mybir

F32 = mybir.dt.float32
F32R = mybir.dt.float32r
ALU = mybir.AluOpType
ACT = mybir.ActivationFunctionType
AX = mybir.AxisListType.X

P = 128
D = 512
S = D // P
ROWS = 32
NB = 64
TB = P // ROWS
NT = NB // TB
GT = 4
G = NT // GT
GB = GT * TB
TOK = GT * P
K = 8
HID = 128
FF = 1792
M = FF // P
E1, RANK, TOP1 = 8, 16, 2
LORA_SCALE = 32.0 / RANK
AR = E1 * RANK + E1
E2 = 64
LOWEST = -3.0e38
E3 = 8
NPAD = 96
TAPS, PAD = 9, 4
CB = 3
ds = bass.ds


def build(nc, A, out):
    ctx = ExitStack()
    with ctx:
        def sb(name, shape, dt=F32):
            return ctx.enter_context(nc.sbuf_tensor(name, shape, dt))

        def sem(name):
            return ctx.enter_context(nc.semaphore(name))

        def views(t, *widths):
            at, out = 0, []
            for w in widths:
                out.append(t[:, at:at + w])
                at += w
            return out

        x_all = sb("x_all", [P, NT, D])
        xs = sb("xs", [P, GT, D])
        cT = sb("cT", [P, S, TOK])
        c_hi = sb("c_hi", [P, S, TOK], F32R)
        c_lo = sb("c_lo", [P, S, TOK], F32R)
        with ExitStack() as first:
            def sb0(name, dt):
                return first.enter_context(nc.sbuf_tensor(name, [P, 2, TOK], dt))

            silu, hff, h_hi, h_lo = sb0("silu", F32), sb0("hff", F32), sb0("h_hi", F32R), sb0("h_lo", F32R)
        c_hi_odd = sb("c_hi_odd", [P, S, TOK], F32R)
        c_lo_odd = sb("c_lo_odd", [P, S, TOK], F32R)
        agg = sb("agg", [P, 3, NT, ROWS])
        prod = sb("prod", [P, GT, K, ROWS])
        blk = sb("blk", [P, GT, P])
        bias_bc = sb("bias_bc", [P, TOK])
        pack_a = sb("pack_a", [P, NB + 3 * HID + 6])
        condT, net_w0, net_b = views(pack_a, NB, 3 * HID, 6)
        pack_d = sb("pack_d", [P, 3 * HID + 3 * K])
        net_w1, net_w2 = views(pack_d, 3 * HID, 3 * K)
        pack_b = sb("pack_b", [NB, 3 * K + P + NT * K + ROWS])
        b2, selrep, jmask, fside = views(pack_b, 3 * K, P, NT * K, ROWS)
        pack_c = sb("pack_c", [P, 3 * K * ROWS + 3 * ROWS + TB + P + ROWS])
        wk, kbias, bmask, ident, cwT = views(pack_c, 3 * K * ROWS, 3 * ROWS, TB, P, ROWS)
        wk = wk.rearrange("p (i k o) -> p i k o", i=3, k=K)
        h1 = sb("h1", [P, 3, NB])
        h2 = sb("h2", [P, 3, NB])
        att = sb("att", [NB, 3, K])
        att_m = sb("att_m", [NB, 3, NT * K])
        att_bc = sb("att_bc", [P, 3, NT * K])
        attT = sb("attT", [P, 3, NB])
        btab = sb("btab", [NB, 4, ROWS])
        st0 = sb("st0", [NB, 2, 3])
        stg = sb("stg", [P, GB, P + 2])
        wconv = sb("wconv", [P, CB, P])
        scrap = sb("scrap", [P, 1])
        ones = sb("ones", [P, P])
        stat = sb("stat", [P, 4, GT])
        m8 = sb("m8", [P, GT, 8])
        t8 = sb("t8", [P, GT, 8])

        with ExitStack() as first:
            wl0 = first.enter_context(nc.sbuf_tensor("wl0", [P, M, 2 * S * P + D], F32R))
        lg = sb("lg", [P, GT, E2])
        ex = sb("ex", [P, GT, E2])
        rest = sb("rest", [P, GT, E2])
        logit = sb("logit", [P, GT, E2])
        war = sb("war", [P, S, AR])
        wbase = sb("wbase", [P, S, D])
        wlb = sb("wlb", [P, D])
        bbase = sb("bbase", [P, D])
        hm = sb("hm", [P, GT, P])
        hmT = sb("hmT", [P, TOK])
        wr2 = sb("wr2", [P, S, NPAD])
        wr3 = sb("wr3", [P, S, NPAD])
        rb2 = sb("rb2", [P, E2])
        eb2 = sb("eb2", [P, D])
        wsg = sb("wsg", [P, S, D])
        bias3 = sb("bias3", [P, D])
        inc3 = sb("inc3", [P, D])
        outc3 = sb("outc3", [P, D])
        t1 = sb("t1", [P, GT, D])
        osc = sb("osc", [P, GT, D])
        wcat = sb("wcat", [P, GT, P])
        rcat = sb("rcat", [P, GT, P])
        eb_hi = sb("eb_hi", [P, D], F32R)
        eb_lo = sb("eb_lo", [P, D], F32R)
        sgn = sb("sgn", [P, S, D], F32R)
        in_w = sb("in_w", [P, D], F32R)
        out_w = sb("out_w", [P, D], F32R)
        wT = sb("wT", [P, TOK], F32R)

        bias_dram = nc.dram_tensor("bias_dram", (NB, 4, ROWS), F32).ap()

        ps = ctx.enter_context(nc.psum_tensor("ps", [P, 8, 512], F32))

        def bank(i):
            return ps[:, i, :]

        def halves(g):
            return (c_hi_odd, c_lo_odd) if g % 2 else (c_hi, c_lo)

        terms = silu[:, 0]
        prod0 = hff[:].rearrange("p b (j k o) -> p (b j) k o", k=K, o=ROWS)

        s_pack_a = sem("s_pack_a")
        s_pack_b = sem("s_pack_b")
        s_pack_c = sem("s_pack_c")
        s_pack_d = sem("s_pack_d")
        s_x = sem("s_x")
        s_slice = [sem(f"s_slice{m}") for m in range(M)]
        s_wconv = sem("s_wconv")
        s_weights1 = sem("s_weights1")
        s_weights23 = sem("s_weights23")
        s_pad = sem("s_pad")
        s_set = sem("s_set")
        s_mlp = sem("s_mlp")
        s_gelu = sem("s_gelu")
        s_att = sem("s_att")
        s_aexp = sem("s_aexp")
        s_att_spread = sem("s_att_spread")
        s_att_bc = sem("s_att_bc")
        s_att_turned = sem("s_att_turned")
        s_attT = sem("s_attT")
        s_terms = sem("s_terms")
        s_bias0 = sem("s_bias0")
        s_mix0 = sem("s_mix0")
        s_blk_half = sem("s_blk_half")
        s_bias_mm = sem("s_bias_mm")
        s_btab = sem("s_btab")
        s_bias_dram = sem("s_bias_dram")
        s_dve_step = sem("s_dve_step")
        s_pool_step = sem("s_pool_step")
        s_staged = [sem(f"s_staged{i}") for i in range(4)]
        s_bias_bc = [sem(f"s_bias_bc{i}") for i in range(4)]
        s_blk = [sem(f"s_blk{i}") for i in range(4)]
        s_cond_mm = [sem(f"s_cond_mm{i}") for i in range(4)]
        s_cT = [sem(f"s_cT{i}") for i in range(4)]
        s_product = [sem(f"s_product{i}") for i in range(4)]
        s_x_new = [sem(f"s_x_new{i}") for i in range(4)]
        s_c_hi = sem("s_c_hi")
        s_c_lo_even = sem("s_c_lo_even")
        s_c_lo_odd = sem("s_c_lo_odd")
        s_gate = sem("s_gate")
        s_up = sem("s_up")
        s_silu = sem("s_silu")
        s_h = sem("s_h")
        s_h_hi = sem("s_h_hi")
        s_h_lo = sem("s_h_lo")
        s_lora_a = sem("s_lora_a")
        s_shifted1 = sem("s_shifted1")
        s_exp1 = sem("s_exp1")
        s_hm = sem("s_hm")
        s_hm_turned = sem("s_hm_turned")
        s_hmT = sem("s_hmT")
        s_base_bias = sem("s_base_bias")
        s_w_hi = sem("s_w_hi")
        s_w_lo = sem("s_w_lo")
        s_router2 = sem("s_router2")
        s_shifted2 = sem("s_shifted2")
        s_exp2 = sem("s_exp2")
        s_wcat = sem("s_wcat")
        s_share = sem("s_share")
        s_wcat_turned = sem("s_wcat_turned")
        s_wT2 = sem("s_wT2")
        s_c_back = sem("s_c_back")
        s_t1 = sem("s_t1")
        s_t1_added = sem("s_t1_added")
        s_router3 = sem("s_router3")
        s_shifted3 = sem("s_shifted3")
        s_exp3 = sem("s_exp3")
        s_rcat = sem("s_rcat")
        s_rcat_turned = sem("s_rcat_turned")
        s_wT3 = sem("s_wT3")
        s_in_scale = sem("s_in_scale")
        s_out_scale = sem("s_out_scale")
        s_osc = sem("s_osc")
        s_scaled = sem("s_scaled")
        s_scaled_hi = sem("s_scaled_hi")
        s_scaled_lo_even = sem("s_scaled_lo_even")
        s_scaled_lo_odd = sem("s_scaled_lo_odd")
        s_bias3 = sem("s_bias3")
        s_rescaled = sem("s_rescaled")
        s_tail = sem("s_tail")
        s_out = sem("s_out")

        block = ctx.enter_context(nc.Block())

        COND = {0: 0, 2: 1, 3: 2}
        UPPER, SPARING = [4, 5, 6, 7], [5, 6, 7, 5]
        IN_BANKS0, EARLY, LATE = [4, 5, 2, 3], (2, 3), (0, 1)
        STG = 16 * S * TB

        @block.sync
        def _(sp):
            xd = A["x"].rearrange("(j p) n -> p j n", p=P)
            od = out.rearrange("(j p) n -> p j n", p=P)
            sp.dma_start(pack_a[:], A["pack_a"]).then_inc(s_pack_a, 16)
            sp.dma_start(pack_d[:], A["pack_d"]).then_inc(s_pack_d, 16)
            sp.dma_start(pack_c[:], A["pack_c"]).then_inc(s_pack_c, 16)
            sp.dma_start(xs[:], xd[:, 0:GT, :]).then_inc(s_staged[0], 16)

            def bias(l, g):
                if l > 0 or g > 0:
                    before, done = (l, g * S) if g else (l - 1, G * S)
                    sp.wait_ge(s_cT[before], done)
                src = bias_dram[g * GB:(g + 1) * GB, l, :].unsqueeze(0).broadcast_to([P, GB, ROWS])
                sp.dma_start(bias_bc[:].rearrange("p (b o) -> p b o", o=ROWS), src).then_inc(s_bias_bc[l], 16)

            def regroup(g):
                sp.wait_ge(s_x_new[0], (g + 1) * GT)
                if g:
                    sp.wait_ge(s_cond_mm[1], g * GT)
                for s in range(S):
                    for b in range(TB):
                        src = x_all[b * ROWS:(b + 1) * ROWS, g * GT:(g + 1) * GT, s * P:(s + 1) * P]
                        dst = stg[s * ROWS:(s + 1) * ROWS, b:GB:TB, 1:P + 1]
                        sp.dma_start(dst, src).then_inc(s_staged[1], 16)

            def stage(g):
                before, done = (2, g * S) if g else (0, G * S)
                sp.wait_ge(s_cond_mm[before], done)
                sp.wait_ge(s_x_new[1], (g + 1) * GT)
                sp.dma_start(xs[:], x_all[:, g * GT:(g + 1) * GT, :]).then_inc(s_staged[2], 16)

            sp.wait_ge(s_btab, 2)
            sp.dma_start(bias_dram, btab[:]).then_inc(s_bias_dram, 16)
            sp.wait_ge(s_bias_dram, 16)
            sp.wait_ge(s_slice[M - 1], 16)
            sp.dma_start(x_all[:], xd).then_inc(s_x, 16)
            sp.dma_start(wconv[:], A["wconv"]).then_inc(s_wconv, 16)
            for g in range(1, G):
                bias(0, g)
                sp.wait_ge(s_cond_mm[0], g * S)
                sp.dma_start(xs[:], xd[:, g * GT:(g + 1) * GT, :]).then_inc(s_staged[0], 16)
                if g == 1:
                    sp.wait_ge(s_pad, 1)
                    regroup(0)
            bias(1, 0)
            sp.wait_ge(s_up, G * M)
            for dst, src in ((war, "war"), (wbase, "wbase"), (bbase, "bbase"), (wlb, "wlb")):
                sp.dma_start(dst[:], A[src]).then_inc(s_weights1, 16)
            for dst, src in ((eb2, "eb2"), (inc3, "inc3"), (outc3, "outc3"), (wsg, "wsg"),
                             (wr2, "wr2"), (rb2, "rb2"), (wr3, "wr3"), (bias3, "bias3")):
                sp.dma_start(dst[:], A[src]).then_inc(s_weights23, 16)
            for g in range(1, G):
                regroup(g)
                bias(1, g)
            for g in range(G):
                stage(g)
                bias(2, g)
            for g in range(G):
                bias(3, g)
            for g in range(G):
                for j in range(g * GT, (g + 1) * GT):
                    sp.wait_ge(s_x_new[3], j + 1)
                    if j == NT - 1:
                        sp.wait_ge(s_tail, 1)
                    sp.dma_start(od[:, j, :], x_all[:, j, :]).then_inc(s_out, 16)
            sp.wait_ge(s_out, 16 * NT)

        @block.gpsimd
        def _(pool):
            pool.memset(stg[:, :, 0:P + 2:P + 1], 0.0).then_inc(s_pad, 1)

            def weights(m0, m1):
                for m in range(m0, m1):
                    pool.dma_start(wl0[:, m, :], A["wl0"][m]).then_inc(s_slice[m], 16)

            chain = [0]

            def step(ins):
                chain[0] += 1
                ins.then_inc(s_pool_step, 1)
                pool.wait_ge(s_pool_step, chain[0])

            def mix(i, q):
                a = att_bc[:, i, q * GT * K:(q + 1) * GT * K].rearrange("p (j k) -> p j k", k=K)
                step(pool.tensor_tensor(prod[:], a.unsqueeze(3).broadcast_to([P, GT, K, ROWS]),
                                        wk[:, i].unsqueeze(1).broadcast_to([P, GT, K, ROWS]), ALU.mult))
                for n in (4, 2):
                    step(pool.tensor_tensor(prod[:, :, 0:n], prod[:, :, 0:n], prod[:, :, n:2 * n], ALU.add))
                step(pool.tensor_tensor(agg[:, i, q * GT:(q + 1) * GT], prod[:, :, 0], prod[:, :, 1], ALU.add))

            def split_c(g):
                for s in (0, 2):
                    pool.wait_ge(s_c_hi, S * g + s + 1)
                    pool.tensor_tensor(c_lo[:, s], cT[:, s], c_hi[:, s].bitcast(F32),
                                       ALU.subtract).then_inc(s_c_lo_even, 1)

            def block_diagonal(l, g):
                if not isinstance(g, int) or g > 0:
                    pool.wait_ge(s_cond_mm[l], g * S)
                elif l > 0:
                    pool.wait_ge(s_cond_mm[{2: 0, 3: 2}[l]], G * S)
                pool.tensor_tensor(blk[:].rearrange("p j (b o) -> p j b o", b=TB),
                                   agg[:, COND[l], ds(g * GT, GT)].unsqueeze(2).broadcast_to([P, GT, TB, ROWS]),
                                   bmask.unsqueeze(1).unsqueeze(3).broadcast_to([P, GT, TB, ROWS]),
                                   ALU.mult).then_inc(s_blk[l], 1)

            pool.wait_ge(s_pack_d, 16)
            weights(0, 3)
            pool.wait_ge(s_pack_c, 16)
            pool.wait_ge(s_attT, 1)
            pool.tensor_tensor(terms.rearrange("p (b o) -> p b o", o=ROWS),
                               attT[:, 0, 0:GB].unsqueeze(2).broadcast_to([P, GB, ROWS]),
                               kbias[:, 0:ROWS].unsqueeze(1).broadcast_to([P, GB, ROWS]),
                               ALU.mult).then_inc(s_terms, 1)
            split_c(0)
            weights(3, M)
            pool.wait_ge(s_att_bc, 2)
            for q in range(1, G):
                mix(0, q)
            for i in (1, 2):
                for q in range(G):
                    mix(i, q)
            with pool.Fori(1, G) as g:
                block_diagonal(0, g)
                split_c(g)
            block_diagonal(2, 0)

            def base_bias(g):
                pool.wait_ge(s_weights1, 64)
                pool.wait_ge(s_staged[1], STG * (g + 1))
                xg = x_all[:, ds(g * GT, GT), :]
                pool.tensor_tensor(xg, xg, bbase[:].unsqueeze(1).broadcast_to([P, GT, D]),
                                   ALU.add).then_inc(s_base_bias, 1)

            base_bias(0)
            pool.wait_ge(s_weights23, 16 * 8)
            pool.wait_ge(s_w_hi, 4)
            half = P // 2
            pool.wait_ge(s_base_bias, 1)
            pool.tensor_tensor(eb_lo[:], eb2[:], eb_hi[:].bitcast(F32), ALU.subtract).then_inc(s_w_lo, 1)
            pool.wait_ge(s_w_lo, 1)
            for n, (w, src) in enumerate(((in_w, inc3), (out_w, outc3))):
                pool.tensor_tensor(w[half:P], src[half:P], w[half:P].bitcast(F32), ALU.subtract).then_inc(s_w_lo, 1)
                pool.wait_ge(s_w_lo, n + 2)
            with pool.Fori(1, G) as g:
                base_bias(g)

            def add_scaled(g):
                pool.wait_ge(s_staged[2], (g + 1) * 16)
                for j in range(GT):
                    pool.wait_ge(s_t1, g * GT + j + 1)
                    xg = x_all[:, ds(g * GT + j, 1), :]
                    pool.tensor_tensor(xg, xg, t1[:, j:j + 1, :], ALU.add).then_inc(s_t1_added, 1)

            with pool.Fori(1, G) as g:
                block_diagonal(2, g)
                add_scaled(g - 1)
            block_diagonal(3, 0)
            add_scaled(G - 1)

            def split_x(g):
                hi, lo = halves(g)
                for s in (0, 2):
                    pool.wait_ge(s_scaled_hi, S * g + s + 1)
                    pool.tensor_tensor(lo[:, s], cT[:, s], hi[:, s].bitcast(F32),
                                       ALU.subtract).then_inc(s_scaled_lo_even, 1)

            def bias_3(g):
                pool.wait_ge(s_cond_mm[3], S * (g + 1))
                xg = x_all[:, g * GT:(g + 1) * GT, :]
                pool.tensor_tensor(xg, xg, bias3[:].unsqueeze(1).broadcast_to([P, GT, D]),
                                   ALU.add).then_inc(s_bias3, 1)

            def finish_3(g, js):
                pool.wait_ge(s_bias3, g + 1)
                for j in js:
                    pool.wait_ge(s_rescaled, g * GT + j + 1)
                    xg = x_all[:, g * GT + j, :]
                    pool.tensor_tensor(xg, xg, t1[:, j], ALU.add).then_inc(s_x_new[3], 1)

            block_diagonal(3, 1)
            split_x(0)
            bias_3(0)
            for g in range(G - 1):
                if g + 2 < G:
                    block_diagonal(3, g + 2)
                bias_3(g + 1)
                finish_3(g, range(GT - 1))
                split_x(g + 1)
                finish_3(g, [GT - 1])
            finish_3(G - 1, range(GT - 1))
            pool.wait_ge(s_rescaled, NT)
            xt = x_all[:, NT - 1, 0:D // 2]
            pool.tensor_tensor(xt, xt, t1[:, GT - 1, 0:D // 2], ALU.add).then_inc(s_x_new[3], 1)

        @block.tensor
        def _(pe):
            def mm(o, l, r, start=True, stop=True):
                return pe.matmul(o, l, r, start=start, stop=stop)

            def cols(j):
                return slice(j * P, (j + 1) * P)

            pe.wait_ge(s_pack_a, 16)
            for i in range(3):
                mm(bank(i)[:, 0:NB], net_w0[:, i * HID:(i + 1) * HID], condT).then_inc(s_mlp, 1)
            pe.wait_ge(s_pack_d, 16)
            for i in range(3):
                pe.wait_ge(s_gelu, i + 1)
                mm(bank(3 + i)[:, 0:NB], net_w1[:, i * HID:(i + 1) * HID], h1[:, i]).then_inc(s_mlp, 1)
            for i in range(3):
                pe.wait_ge(s_gelu, 3 + i + 1)
                mm(bank(6)[0:NB, i * K:(i + 1) * K], h2[:, i], net_w2[:, i * K:(i + 1) * K]).then_inc(s_mlp, 1)
            pe.wait_ge(s_set, 2)
            for _ in range(5):
                mm(bank(7)[:, 0:P], ones[:], ones[:])
            pe.wait_ge(s_att, 7)
            mm(bank(3)[:, 0:NT * K], selrep, att_m[:, 0]).then_inc(s_att_spread, 1)
            pe.wait_ge(s_pack_c, 16)
            pe.transpose(bank(0)[:, 0:NB], att_m[:, 0], ident[0:NB, 0:NB]).then_inc(s_att_turned, 1)
            pe.wait_ge(s_att, 9)
            others = att_m[:, 1:3].rearrange("b i n -> b (i n)")
            mm(bank(2)[:, 0:2 * NT * K], selrep, others).then_inc(s_att_spread, 1)
            for i in (1, 2):
                ins = pe.transpose(bank(1)[:, (i - 1) * NB:i * NB], att_m[:, i], ident[0:NB, 0:NB])
            ins.then_inc(s_att_turned, 1)
            pe.wait_ge(s_terms, 1)
            mm(bank(0), ones[:], terms).then_inc(s_bias0, 1)

            def nothing():
                pass

            def cond_chunk(l, g, s, b):
                for j in range(GT):
                    x = x_all[:, g * GT + j, cols(s)] if l == 3 else xs[:, j, cols(s)]
                    ins = mm(bank(b)[:, cols(j)], x, blk[:, j])
                ins.then_inc(s_cond_mm[l], 1)

            def cond(l, g, banks, before):
                if l == 3:
                    pe.wait_ge(s_x_new[2], GT * (g + 1))
                else:
                    pe.wait_ge(s_staged[l], 16 * (g + 1))
                pe.wait_ge(s_blk[l], g + 1)
                for s, b in enumerate(banks):
                    before[s]()
                    cond_chunk(l, g, s, b)

            def gate_up(g, m):
                n = g * M + m
                pe.wait_ge(s_slice[m], 16)
                if m >= 2:
                    pe.wait_ge(s_h, n - 1)
                b = 4 + 2 * (m % 2)
                for u, done in ((0, s_gate), (1, s_up)):
                    passes = [(c, s) for s in range(S) for c in (c_hi, c_lo)]
                    arriving = m == 0 and u == 0
                    if arriving:
                        passes = [(c, s) for c in (c_hi, c_lo) for s in range(S)]
                    for c, s in passes:
                        if arriving and c is c_hi:
                            pe.wait_ge(s_c_hi, S * g + s + 1)
                        if arriving and c is c_lo:
                            pe.wait_ge(s_c_lo_odd if s % 2 else s_c_lo_even, 2 * g + s // 2 + 1)
                        first, last = s == 0 and c is c_hi, s == S - 1 and c is c_lo
                        ins = mm(bank(b + u), wl0[:, m, cols(u * S + s)], c[:, s], first, last)
                    ins.then_inc(done, 1)

            def down(g, m):
                pe.wait_ge(s_h_lo, g * M + m + 1)
                w = wl0[:, m, 2 * S * P:2 * S * P + D]
                for j in range(GT):
                    mm(bank(j), h_hi[:, m % 2, cols(j)], w, start=m == 0, stop=False)
                    ins = mm(bank(j), h_lo[:, m % 2, cols(j)], w, start=False, stop=m == M - 1)
                    if m == M - 1:
                        ins.then_inc(s_product[0], 1)

            def conv(g, j):
                if j == 0:
                    pe.wait_ge(s_staged[1], STG * (g + 1))
                for b in range(TB):
                    for c in range(CB):
                        ins = mm(bank(4 + j)[:, cols(b)], stg[:, j * TB + b, c:c + P], wconv[:, c],
                                 start=c == 0, stop=c == CB - 1)
                ins.then_inc(s_cond_mm[1], 1)

            def layer0(g, more):
                for m in range(M):
                    gate_up(g, m)
                    if m >= 1:
                        down(g, m - 1)
                pe.wait_ge(s_h, g * M + M - 1)
                if more:
                    cond(0, g + 1, UPPER, [nothing, nothing, lambda: pe.wait_ge(s_h, g * M + M), nothing])
                else:
                    pe.wait_ge(s_wconv, 16)
                    for j in range(GT):
                        if j == 2:
                            pe.wait_ge(s_h, g * M + M)
                        conv(0, j)
                down(g, M - 1)

            pe.wait_ge(s_staged[0], 16)
            for ready, js in ((s_blk_half, (0, 1)), (s_blk[0], (2, 3))):
                pe.wait_ge(ready, 1)
                for s in range(S):
                    for j in js:
                        ins = mm(bank(4 + s)[:, cols(j)], xs[:, j, cols(s)], blk[:, j])
                    if 3 in js:
                        ins.then_inc(s_cond_mm[0], 1)
            pe.wait_ge(s_attT, 2)
            for l, i in COND.items():
                mm(bank(1)[0:NB, l * ROWS:(l + 1) * ROWS], attT[:, i], kbias[:, i * ROWS:(i + 1) * ROWS])
            mm(bank(1)[0:NB, ROWS:2 * ROWS], condT, cwT).then_inc(s_bias_mm, 1)
            with pe.Fori(0, G - 1) as g:
                layer0(g, True)
            layer0(G - 1, False)

            def lora_a_router(g):
                pe.wait_ge(s_weights1, 64)
                pe.wait_ge(s_cT[1], GT * g + GT)
                for j in range(GT):
                    for s in range(S):
                        ins = mm(bank(4 + j)[:, 0:AR], cT[:, s, cols(j)], war[:, s], s == 0, s == S - 1)
                ins.then_inc(s_lora_a, 1)

            def base(g):
                for j in range(GT):
                    for s in range(S):
                        mm(bank(j), cT[:, s, cols(j)], wbase[:, s], s == 0, False)

            def turn_hm(g):
                for j in range(GT):
                    ins = pe.transpose(bank(4)[:, cols(j)], hm[:, j], ident)
                ins.then_inc(s_hm_turned, 1)

            def lora_b(g):
                pe.wait_ge(s_hmT, g + 1)
                for j in range(GT):
                    mm(bank(j), hmT[:, cols(j)], wlb[:], False, True).then_inc(s_product[1], 1)

            def layer1(g, more):
                base(g)
                pe.wait_ge(s_hm, g + 1)
                if more:
                    for j in range(GT - 1):
                        conv(g + 1, j)
                    pe.wait_ge(s_cT[1], GT * (g + 1) + 1)
                    turn_hm(g)
                    conv(g + 1, GT - 1)
                    lora_b(g)
                    lora_a_router(g + 1)
                else:
                    cond(2, 0, SPARING, [nothing, nothing, nothing, lambda: (turn_hm(g), pe.wait_ge(s_cT[2], 1))])
                    lora_b(g)
                    pe.wait_ge(s_w_lo, 3)
                    pe.wait_ge(s_weights23, 16 * 8)
                    router2(0)
                pe.wait_ge(s_x_new[1], GT * (g + 1))

            def router2(g):
                pe.wait_ge(s_cT[2], S * (g + 1))
                for j in range(GT):
                    for s in range(S):
                        ins = mm(bank(4)[:, j * P:j * P + NPAD], cT[:, s, cols(j)], wr2[:, s], s == 0, s == S - 1)
                ins.then_inc(s_router2, 1)

            def turn_weights(g):
                pe.wait_ge(s_wcat, g + 1)
                for j in range(GT):
                    ins = pe.transpose(bank(4)[:, cols(j)], wcat[:, j], ident)
                ins.then_inc(s_wcat_turned, 1)

            def layer2(g, more):
                for j in range(GT):
                    for s in range(S):
                        ins = pe.transpose(bank(j)[:, cols(s)], cT[:, s, cols(j)], ident)
                    ins.then_inc(s_c_back, 1)
                l, h = (2, g + 1) if more else (3, 0)
                cond(l, h, SPARING, [nothing, nothing, nothing,
                                      lambda: (turn_weights(g), pe.wait_ge(s_cT[l], S * h + 1))])
                pe.wait_ge(s_wT2, g + 1)
                for j in range(GT):
                    pe.wait_ge(s_t1, GT * g + j + 1)
                    mm(bank(j), wT[:, cols(j)], eb_hi[:], True, False)
                    mm(bank(j), wT[:, cols(j)], eb_lo[:], False, True).then_inc(s_product[2], 1)
                if more:
                    router2(g + 1)
                else:
                    pe.wait_ge(s_w_hi, 4)
                    router3(0)
                pe.wait_ge(s_x_new[2], GT * (g + 1))

            def router3(g):
                pe.wait_ge(s_cT[3], S * (g + 1))
                for j in range(GT):
                    for s in range(S):
                        ins = mm(bank(4)[:, j * P:j * P + NPAD], cT[:, s, cols(j)], wr3[:, s], s == 0, s == S - 1)
                ins.then_inc(s_router3, 1)

            def sign_product(g, j, chunks=range(S)):
                hi, lo = halves(g)
                if chunks[0] == 0:
                    pe.wait_ge(s_osc, GT * g + j + 1)
                passes = [(part, s) for s in chunks for part in (hi, lo)]
                if j == 0:
                    passes = [(part, s) for part in (hi, lo) for s in chunks]
                for part, s in passes:
                    if j == 0 and part is hi:
                        pe.wait_ge(s_scaled_hi, S * g + s + 1)
                    if j == 0 and part is lo:
                        pe.wait_ge(s_scaled_lo_odd if s % 2 else s_scaled_lo_even, 2 * g + s // 2 + 1)
                    first, last = s == 0 and part is hi, s == S - 1 and part is lo
                    ins = mm(bank(j), part[:, s, cols(j)], sgn[:, s], first, last)
                if last:
                    ins.then_inc(s_product[3], 1)

            def turn_routing(g):
                pe.wait_ge(s_rcat, g + 1)
                for j in range(GT):
                    ins = pe.transpose(bank(5)[:, cols(j)], rcat[:, j], ident)
                ins.then_inc(s_rcat_turned, 1)

            def in_scales(g):
                pe.wait_ge(s_wT3, g + 1)
                for s in range(S):
                    mm(bank(4 + s if g else IN_BANKS0[s]), in_w[:, cols(s)], wT[:]).then_inc(s_in_scale, 1)

            def out_scales(g, js=range(GT)):
                for j in js:
                    if g == 0 and j in IN_BANKS0:
                        pe.wait_ge(s_scaled, IN_BANKS0.index(j) + 1)
                    if g:
                        pe.wait_ge(s_rescaled, GT * (g - 1) + j + 1)
                    mm(bank(j), wT[:, cols(j)], out_w[:]).then_inc(s_out_scale, 1)

            def cond3(g):
                cond(3, g, UPPER, [(lambda s=s: pe.wait_ge(s_scaled, S * (g - 1) + s + 1)) for s in range(S)])

            lora_a_router(0)
            pe.wait_ge(s_x_new[0], G * GT)
            with pe.Fori(0, G - 1) as g:
                layer1(g, True)
            layer1(G - 1, False)
            with pe.Fori(0, G - 1) as g:
                layer2(g, True)
            layer2(G - 1, False)
            pe.wait_ge(s_x_new[2], 2 * GT)
            pe.wait_ge(s_blk[3], 2)
            for s in EARLY:
                cond_chunk(3, 1, s, 4 + s)
            turn_routing(0)
            in_scales(0)
            out_scales(0, (0, 1))
            for s in LATE:
                pe.wait_ge(s_scaled, s + 1)
                cond_chunk(3, 1, s, 4 + s)
            out_scales(0, (2, 3))
            for g in range(G - 1):
                sign_product(g, 0)
                router3(g + 1)
                sign_product(g, 1)
                sign_product(g, 2)
                turn_routing(g + 1)
                sign_product(g, 3, (0, 1))
                in_scales(g + 1)
                sign_product(g, 3, (2, 3))
                out_scales(g + 1)
                if g + 2 < G:
                    cond3(g + 2)
            for j in range(GT):
                sign_product(G - 1, j)

        @block.scalar
        def _(act):
            def copy(o, i):
                return act.activation(o, i, ACT.Copy)

            act.dma_start(pack_b[:], A["pack_b"]).then_inc(s_pack_b, 16)
            act.wait_ge(s_set, 1)
            act.activation(scrap[:], scrap[:], ACT.Gelu)
            act.wait_ge(s_pack_a, 16)
            for n, dst in enumerate((h1, h2)):
                for i in range(3):
                    at = 3 * n + i
                    act.wait_ge(s_mlp, at + 1)
                    act.activation(dst[:, i], bank(at)[:, 0:NB], ACT.Gelu,
                                   bias=net_b[:, at:at + 1]).then_inc(s_gelu, 1)
            act.wait_ge(s_att, 3)
            act.activation(att[:], att[:], ACT.Exp).then_inc(s_aexp, 1)
            act.wait_ge(s_att_turned, 1)
            copy(attT[:, 0], bank(0)[:, 0:NB]).then_inc(s_attT, 1)
            act.wait_ge(s_att_turned, 2)
            copy(attT[:, 1:3].rearrange("p i n -> p (i n)"), bank(1)[:, 0:2 * NB]).then_inc(s_attT, 1)
            act.activation(scrap[:], scrap[:], ACT.Silu)
            act.wait_ge(s_bias0, 1)
            copy(bias_bc[:], bank(0)).then_inc(s_bias_bc[0], 16)
            copy(att_bc[:, 1:3].rearrange("p i n -> p (i n)"), bank(2)[:, 0:2 * NT * K]).then_inc(s_att_bc, 1)
            act.wait_ge(s_mix0, 3)
            copy(att_bc[:, 0], bank(3)[:, 0:NT * K]).then_inc(s_att_bc, 1)

            def split_c(g):
                for s in range(S):
                    act.wait_ge(s_cT[0], S * g + s + 1)
                    copy(c_hi[:, s], cT[:, s]).then_inc(s_c_hi, 1)

            def layer0(g, more):
                for m in range(M):
                    n = g * M + m
                    act.wait_ge(s_gate, n + 1)
                    act.activation(silu[:, m % 2], bank(4 + 2 * (m % 2)), ACT.Silu).then_inc(s_silu, 1)
                    act.wait_ge(s_h, n + 1)
                    copy(h_hi[:, m % 2], hff[:, m % 2]).then_inc(s_h_hi, 1)
                if more:
                    split_c(g + 1)

            split_c(0)
            act.wait_ge(s_bias_mm, 1)
            copy(btab[:].rearrange("b l o -> b (l o)"), bank(1)[0:NB, 0:4 * ROWS]).then_inc(s_btab, 1)
            with act.Fori(0, G - 1) as g:
                layer0(g, True)
            layer0(G - 1, False)

            act.wait_ge(s_weights23, 16 * 8)
            act.wait_ge(s_product[0], G * GT)
            for dst, src in ((eb_hi, eb2), (in_w, inc3), (out_w, outc3)):
                copy(dst[:], src[:]).then_inc(s_w_hi, 1)
            act.activation(sgn[:], wsg[:], ACT.Sign).then_inc(s_w_hi, 1)

            def exp(s_ready, s_done, g, width):
                act.wait_ge(s_ready, g + 1)
                act.activation(ex[:, :, 0:width], lg[:, :, 0:width], ACT.Exp).then_inc(s_done, 1)

            with act.Fori(0, G) as g:
                exp(s_shifted1, s_exp1, g, E1)
                act.wait_ge(s_hm_turned, g + 1)
                copy(hmT[:], bank(4)).then_inc(s_hmT, 1)

            def scaled(g, j):
                act.wait_ge(s_c_back, GT * g + j + 1)
                act.activation(t1[:, j], bank(j), ACT.Copy, scale=stat[:, 3, j:j + 1]).then_inc(s_t1, 1)

            def layer2(g, more):
                exp(s_shifted2, s_exp2, g, E2)
                act.wait_ge(s_share, g + 1)
                scaled(g, 0)
                scaled(g, 1)
                act.wait_ge(s_wcat_turned, g + 1)
                copy(wT[:], bank(4)).then_inc(s_wT2, 1)
                scaled(g, 2)
                scaled(g, 3)
                if more:
                    act.wait_ge(s_t1_added, GT * (g + 1))

            with act.Fori(0, G - 1) as g:
                layer2(g, True)
            layer2(G - 1, False)

            for g in range(G):
                exp(s_shifted3, s_exp3, g, E3)
                act.wait_ge(s_rcat_turned, g + 1)
                copy(wT[:], bank(5)).then_inc(s_wT3, 1)

                def high(n):
                    act.wait_ge(s_scaled, S * g + n + 1)
                    copy(halves(g)[0][:, n], cT[:, n]).then_inc(s_scaled_hi, 1)

                def out_scale(j):
                    act.wait_ge(s_out_scale, GT * g + j + 1)
                    copy(osc[:, j], bank(j)).then_inc(s_osc, 1)

                high(0)
                high(1)
                out_scale(0)
                high(2)
                high(3)
                for j in range(1, GT):
                    out_scale(j)

        @block.vector
        def _(dve):
            def tt(o, a, b, op):
                return dve.tensor_tensor(o, a, b, op)

            dve.memset(scrap[:], 0.0).then_inc(s_set, 1)
            dve.memset(ones[:], 1.0).then_inc(s_set, 1)
            flat = att[:].rearrange("b i k -> b (i k)")
            dve.wait_ge(s_pack_b, 16)
            dve.wait_ge(s_mlp, 9)
            tt(flat, bank(6)[0:NB, 0:3 * K], b2, ALU.add).then_inc(s_att, 1)
            dve.wait_ge(s_att, 1)
            dve.tensor_reduce(st0[:, 0], att[:], AX, ALU.max).then_inc(s_att, 1)
            dve.wait_ge(s_att, 2)
            tt(att[:], att[:], st0[:, 0].unsqueeze(2).broadcast_to([NB, 3, K]), ALU.subtract).then_inc(s_att, 1)
            dve.wait_ge(s_aexp, 1)
            dve.tensor_reduce(st0[:, 0], att[:], AX, ALU.add).then_inc(s_att, 1)
            dve.wait_ge(s_att, 4)
            dve.reciprocal(st0[:, 1], st0[:, 0]).then_inc(s_att, 1)
            dve.wait_ge(s_att, 5)
            tt(att[:], att[:], st0[:, 1].unsqueeze(2).broadcast_to([NB, 3, K]), ALU.mult).then_inc(s_att, 1)
            dve.wait_ge(s_att, 6)
            for i in range(3):
                tt(att_m[:, i].rearrange("b (j k) -> b j k", k=K), jmask.rearrange("b (j k) -> b j k", k=K),
                   att[:, i].unsqueeze(1).broadcast_to([NB, NT, K]), ALU.mult).then_inc(s_att, 1)
            dve.wait_ge(s_pack_c, 16)
            dve.wait_ge(s_att_spread, 1)
            for n in range(2):
                js = slice(n * GT // 2, (n + 1) * GT // 2)
                a = bank(3)[:, 0:GT * K].rearrange("p (j k) -> p j k", k=K)[:, js]
                half = [P, GT // 2, K, ROWS]
                tt(prod0[:, js], a.unsqueeze(3).broadcast_to(half), wk[:, 0].unsqueeze(1).broadcast_to(half),
                   ALU.mult).then_inc(s_mix0, 1)
                dve.wait_ge(s_mix0, 2 * n + 1)
                dve.tensor_reduce(agg[:, 0, js], prod0[:, js].rearrange("p j k o -> p j o k"), AX,
                                  ALU.add).then_inc(s_mix0, 1)
                dve.wait_ge(s_mix0, 2 * n + 2)
                half = [P, GT // 2, TB, ROWS]
                tt(blk[:, js].rearrange("p j (b o) -> p j b o", b=TB), agg[:, 0, js].unsqueeze(2).broadcast_to(half),
                   bmask.unsqueeze(1).unsqueeze(3).broadcast_to(half),
                   ALU.mult).then_inc(s_blk_half if n == 0 else s_blk[0], 1)

            def cond(l, g, banks):
                dve.wait_ge(s_bias_bc[l], 16 * (g + 1))
                for s in range(S):
                    dve.wait_ge(s_cond_mm[l], S * g + s + 1)
                    tt(cT[:, s], bank(banks[s]), bias_bc[:], ALU.add).then_inc(s_cT[l], 1)

            def cond1(g):
                dve.wait_ge(s_bias_bc[1], 16 * (g + 1))
                v = bias_bc[:].rearrange("p (b o) -> p b o", o=ROWS)
                for j in range(GT):
                    dve.wait_ge(s_cond_mm[1], GT * g + j + 1)
                    o = cT[:, :, j * P:(j + 1) * P].rearrange("p s (b o) -> p b s o", o=ROWS)
                    tt(o, bank(4 + j).rearrange("p (b s o) -> p b s o", b=TB, s=S),
                       v[:, j * TB:(j + 1) * TB].unsqueeze(2).broadcast_to([P, TB, S, ROWS]),
                       ALU.add).then_inc(s_cT[1], 1)

            def residual(l, g):
                for j in range(GT):
                    dve.wait_ge(s_product[l], GT * g + j + 1)
                    xt = x_all[:, ds(g * GT + j, 1), :]
                    tt(xt, xt, bank(j).unsqueeze(1), ALU.add).then_inc(s_x_new[l], 1)

            def split_c(g):
                for s in (1, 3):
                    dve.wait_ge(s_c_hi, S * g + s + 1)
                    tt(c_lo[:, s], cT[:, s], c_hi[:, s].bitcast(F32), ALU.subtract).then_inc(s_c_lo_odd, 1)

            def layer0(g, more):
                for m in range(M):
                    n = g * M + m
                    dve.wait_ge(s_silu, n + 1)
                    dve.wait_ge(s_up, n + 1)
                    tt(hff[:, m % 2], silu[:, m % 2], bank(5 + 2 * (m % 2)), ALU.mult).then_inc(s_h, 1)
                    dve.wait_ge(s_h_hi, n + 1)
                    tt(h_lo[:, m % 2], hff[:, m % 2], h_hi[:, m % 2].bitcast(F32), ALU.subtract).then_inc(s_h_lo, 1)
                if more:
                    cond(0, g + 1, UPPER)
                    split_c(g + 1)
                else:
                    cond1(0)
                dve.wait_ge(s_x, 16)
                residual(0, g)

            cond(0, 0, UPPER)
            split_c(0)
            dve.wait_ge(s_btab, 1)
            tt(btab[:, 1], btab[:, 1], fside, ALU.add).then_inc(s_btab, 1)
            with dve.Fori(0, G - 1) as g:
                layer0(g, True)
            layer0(G - 1, False)

            def bc(v, n):
                return v.unsqueeze(2).broadcast_to([P, GT, n])

            def alone():
                dve.memset(scrap[:], 0.0)

            def linker(base, per, g):
                n = [0]

                def link(ins, apart=False):
                    n[0] += 1
                    ins.then_inc(s_dve_step, 1)
                    dve.wait_ge(s_dve_step, base + per * g + n[0])
                    if apart:
                        alone()
                link.count = n
                return link

            PER1, PER2, PER3 = 9, 6, 6
            base2 = PER1 * G
            base3 = base2 + PER2 * G

            def route1(g):
                link = linker(0, PER1, g)
                e, c = ex[:, :, 0:E1], lg[:, :, 0:E1]
                head = ps[:, 4:8, E1 * RANK:AR]
                dve.wait_ge(s_lora_a, g + 1)
                link(dve.tensor_reduce(stat[:, 0], head, AX, ALU.max))
                tt(c, head, bc(stat[:, 0], E1), ALU.subtract).then_inc(s_shifted1, 1)
                dve.wait_ge(s_exp1, g + 1)
                alone()
                for j in range(GT):
                    ins = dve.max(m8[:, j], ex[:, j, 0:E1])
                link(ins)
                link(dve.tensor_copy(t8[:, :, 0:TOP1], m8[:, :, 0:TOP1]), True)
                for j in range(GT):
                    ins = dve.match_replace(rest[:, j, 0:E1], t8[:, j], ex[:, j, 0:E1], 0.0)
                link(ins)
                link(tt(stat[:, 1], m8[:, :, 0], m8[:, :, 1], ALU.add))
                link(tt(c, e, rest[:, :, 0:E1], ALU.subtract))
                link(dve.reciprocal(stat[:, 2], stat[:, 1]))
                link(dve.tensor_scalar(stat[:, 2], stat[:, 2], LORA_SCALE, None, ALU.mult))
                link(tt(c, c, bc(stat[:, 2], E1), ALU.mult))
                assert link.count[0] == PER1
                h = ps[:, 4:8, 0:E1 * RANK].rearrange("p j (e r) -> p j e r", r=RANK)
                tt(hm[:].rearrange("p j (e r) -> p j e r", r=RANK), h,
                   c.unsqueeze(3).broadcast_to([P, GT, E1, RANK]), ALU.mult).then_inc(s_hm, 1)

            dve.memset(t8[:], -1.0).then_inc(s_set, 1)
            dve.wait_ge(s_set, 3)
            with dve.Fori(0, G - 1) as g:
                route1(g)
                cond1(g + 1)
                dve.wait_ge(s_base_bias, g + 1)
                residual(1, g)
            route1(G - 1)
            cond(2, 0, SPARING)
            dve.wait_ge(s_base_bias, G)
            residual(1, G - 1)

            def route2(g):
                link = linker(base2, PER2, g)
                dve.wait_ge(s_router2, g + 1)
                lt = bank(4).rearrange("p (j e) -> p j e", j=GT)[:, :, 0:E2]
                link(tt(logit[:], lt, rb2[:].unsqueeze(1).broadcast_to([P, GT, E2]), ALU.add), True)
                for j in range(GT):
                    ins = dve.max(m8[:, j], logit[:, j])
                link(ins)
                tt(lg[:], logit[:], bc(m8[:, :, 0], E2), ALU.subtract).then_inc(s_shifted2, 1)
                for j in range(GT):
                    ins = dve.match_replace(rest[:, j], m8[:, j], logit[:, j], LOWEST)
                link(ins)
                link(tt(rest[:], rest[:], logit[:], ALU.not_equal))
                dve.wait_ge(s_exp2, g + 1)
                dve.tensor_reduce(stat[:, 1], ex[:], AX, ALU.add)
                link(tt(lg[:], ex[:], rest[:], ALU.mult))
                dve.reciprocal(stat[:, 2], stat[:, 1])
                dve.tensor_reduce(stat[:, 0], lg[:], AX, ALU.add)
                link(dve.tensor_copy(wcat[:, :, 0:E2].bitcast(F32R), lg[:]))
                tt(stat[:, 3], stat[:, 0], stat[:, 2], ALU.mult).then_inc(s_share, 1)
                tt(wcat[:, :, E2:2 * E2], lg[:], wcat[:, :, 0:E2], ALU.subtract).then_inc(s_wcat, 1)
                assert link.count[0] == PER2

            def final2(g):
                for j in range(GT):
                    dve.wait_ge(s_product[2], GT * g + j + 1)
                    dve.wait_ge(s_t1_added, GT * g + j + 1)
                    xt = x_all[:, ds(g * GT + j, 1), :]
                    dve.scalar_tensor_tensor(xt, bank(j).unsqueeze(1), stat[:, 2, j:j + 1], xt, ALU.mult,
                                             ALU.add).then_inc(s_x_new[2], 1)

            with dve.Fori(0, G - 1) as g:
                route2(g)
                cond(2, g + 1, SPARING)
                final2(g)
            route2(G - 1)
            dve.memset(rcat[:], 0.0)
            cond(3, 0, SPARING)
            final2(G - 1)

            def route3(g):
                link = linker(base3, PER3, g)
                dve.wait_ge(s_router3, g + 1)
                lt = bank(4).rearrange("p (j e) -> p j e", j=GT)[:, :, 0:E3]
                e = ex[:, :, 0:E3]
                link(dve.tensor_reduce(stat[:, 0], lt, AX, ALU.max))
                tt(lg[:, :, 0:E3], lt, bc(stat[:, 0], E3), ALU.subtract).then_inc(s_shifted3, 1)
                dve.wait_ge(s_exp3, g + 1)
                link(dve.tensor_reduce(stat[:, 1], e, AX, ALU.add))
                link(dve.reciprocal(stat[:, 2], stat[:, 1]))
                link(tt(e, e, bc(stat[:, 2], E3), ALU.mult))
                r4 = rcat[:].rearrange("p j (q k) -> p j q k", q=4)
                for q in (0, 2):
                    ins = dve.tensor_copy(r4[:, :, q, 0:E3].bitcast(F32R), e)
                link(ins)
                link(tt(r4[:, :, 1, 0:E3], e, r4[:, :, 0, 0:E3], ALU.subtract))
                assert link.count[0] == PER3
                tt(r4[:, :, 3, 0:E3], e, r4[:, :, 0, 0:E3], ALU.subtract).then_inc(s_rcat, 1)

            def scale_in(g, chunks):
                for s in chunks:
                    dve.wait_ge(s_in_scale, S * g + s + 1)
                    tt(cT[:, s], cT[:, s], bank(4 + s if g else IN_BANKS0[s]), ALU.mult).then_inc(s_scaled, 1)

            def split_x(g, s):
                hi, lo = halves(g)
                dve.wait_ge(s_scaled_hi, S * g + s + 1)
                tt(lo[:, s], cT[:, s], hi[:, s].bitcast(F32), ALU.subtract).then_inc(s_scaled_lo_odd, 1)

            def scale_out(g, js):
                for j in js:
                    dve.wait_ge(s_product[3], GT * g + j + 1)
                    if g:
                        dve.wait_ge(s_x_new[3], GT * (g - 1) + j + 1)
                    tt(t1[:, j], osc[:, j], bank(j), ALU.mult).then_inc(s_rescaled, 1)

            def cond3(g, chunks):
                dve.wait_ge(s_bias_bc[3], 16 * (g + 1))
                for s in chunks:
                    n = (EARLY + LATE).index(s) if g == 1 else s
                    dve.wait_ge(s_cond_mm[3], S * g + n + 1)
                    dve.wait_ge(s_scaled_lo_odd if s % 2 else s_scaled_lo_even, 2 * (g - 1) + s // 2 + 1)
                    tt(cT[:, s], bank(4 + s), bias_bc[:], ALU.add).then_inc(s_cT[3], 1)

            for g in range(G):
                if g:
                    scale_out(g - 1, range(1))
                route3(g)
                if g:
                    scale_out(g - 1, range(1, GT - 1))
                scale_in(g, (0, 1))
                if g:
                    scale_out(g - 1, range(GT - 1, GT))
                scale_in(g, (2, 3))
                split_x(g, 1)
                if g == 0:
                    cond3(1, (0, 1))
                split_x(g, 3)
                if g + 1 < G:
                    cond3(g + 1, range(2 if g == 0 else 0, S))
            scale_out(G - 1, range(GT))
            dve.wait_ge(s_bias3, G)
            dve.wait_ge(s_rescaled, NT)
            xt = x_all[:, NT - 1, D // 2:D]
            tt(xt, xt, t1[:, GT - 1, D // 2:D], ALU.add).then_inc(s_tail, 1)


def kernel(**inputs):
    import numpy as np
    import concourse.bacc as bacc
    from concourse.bass_utils import run_bass_kernel_spmd as launch

    v = {n: np.asarray(a) for n, a in inputs.items()}

    def cols(a):
        return a.reshape(*a.shape[:-1], P, S).swapaxes(-1, -2).reshape(a.shape)

    def rows(a):
        return a.reshape(P, S, a.shape[-1])

    def everywhere(a):
        return np.broadcast_to(a, (P, *a.shape))

    conds = ("L0_cond_", "L2_cond_", "L3_cond_")

    def nets(what):
        return [v[c + what] for c in conds]

    def padded(a, n):
        o = np.zeros((*a.shape[:-1], n), a.dtype)
        o[..., :a.shape[-1]] = a
        return o

    b2 = np.broadcast_to(np.concatenate([v[c + "b2"] for c in conds]), (NB, 3 * K))
    wk = np.stack([np.tile(v[c + "weight"][..., 0].transpose(2, 0, 1), (TB, 1, 1)) for c in conds], 1)
    kbias = np.stack([np.tile(v[c + "bias_k"], (NT, 1)) for c in conds], 1)
    bmask = np.repeat(np.eye(TB, dtype=np.float32), ROWS, 0)
    selrep = np.zeros((NB, TB, ROWS), np.float32)
    selrep[np.arange(NB), np.arange(NB) % TB] = 1
    jmask = np.zeros((NB, NT, K), np.float32)
    jmask[np.arange(NB), np.arange(NB) // TB] = 1
    cw = v["L1_cond_weight"]
    wconv = np.zeros((S, ROWS, CB, S, ROWS), np.float32)
    ig = cw.shape[1]
    for r in range(S):
        for tap in range(TAPS):
            at = r + tap - PAD + S
            for o in range(ROWS):
                i0 = o // ig * ig
                wconv[at % S, i0:i0 + ig, at // S, r, o] = cw[o, :, tap]

    def four(a):
        o = np.zeros((4, P // 4, a.shape[1]), a.dtype)
        o[:, :a.shape[0]] = a
        return o.reshape(P, -1)

    gu = np.stack([v["L0_ffn_W_gate"], v["L0_ffn_W_up"]])
    gu = gu.reshape(2, M, P, P, S).transpose(1, 3, 0, 4, 2).reshape(M, P, 2 * S * P)
    dn = cols(np.ascontiguousarray(v["L0_ffn_W_down"].T)).reshape(M, P, D)

    def beside(*parts):
        return np.concatenate([a.reshape(a.shape[0], -1) for a in parts], 1)

    a_r = np.concatenate([v["L1_ffn_A_stack"].reshape(E1 * RANK, D), v["L1_ffn_W_router"]])
    host = {
        "x": cols(v["x"].reshape(NB * ROWS, D)),
        "pack_a": beside(v["cond_128"].T, *nets("W0"), *nets("b0"), *nets("b1")),
        "pack_d": beside(*nets("W1"), *nets("W2")),
        "pack_b": beside(b2, selrep, jmask, np.broadcast_to(v["fside_S_0"], (NB, ROWS))),
        "pack_c": beside(wk, kbias, bmask, np.eye(P, dtype=np.float32), v["L1_cond_c_weight"].T),
        "bbase": everywhere(cols(v["L1_ffn_b_base"])), "wl0": np.concatenate([gu, dn], 2),
        "wconv": wconv.reshape(P, CB, P), "wbase": cols(rows(v["L1_ffn_W_base"].T)), "war": rows(a_r.T),
        "wlb": cols(v["L1_ffn_B_stack"].transpose(0, 2, 1).reshape(E1 * RANK, D)),
        "wr2": padded(rows(v["L2_ffn_router_weight"].T), NPAD), "rb2": everywhere(v["L2_ffn_router_bias"]),
        "eb2": np.tile(cols(v["L2_ffn_expert_bias"]), (2, 1)),
        "wr3": padded(rows(v["L3_ffn_gate_w"].T), NPAD),
        "wsg": cols(rows(v["L3_ffn_weight"].T)), "bias3": everywhere(cols(v["L3_ffn_bias"])),
        "inc3": four(cols(v["L3_ffn_in_channel_scale"])), "outc3": four(cols(v["L3_ffn_out_channel_scale"])),
    }
    nc = bacc.Bacc("TRN2", target_bir_lowering=False, num_devices=1)
    arrays, aps = {}, {}
    for name, a in host.items():
        a = np.ascontiguousarray(a)
        arrays["in_" + name] = a
        aps[name] = nc.dram_tensor("in_" + name, a.shape, mybir.dt.from_np(a.dtype), kind="ExternalInput").ap()
    out = nc.dram_tensor("out_x", (NB * ROWS, D), F32, kind="ExternalOutput").ap()
    build(nc, aps, out)
    r = launch(nc, [arrays], core_ids=[0])
    y = np.asarray(r.results[0]["out_x"])
    return np.ascontiguousarray(y.reshape(NB * ROWS, S, P).swapaxes(-1, -2)).reshape(NB, ROWS, D)
```
